# Optimizing a Trainium2 kernel written in Bass

```python
import numpy as np
import jax
import jax.numpy as jnp

def _softmax(x, axis=-1):
    return jax.nn.softmax(x, axis=axis)

def _gelu(x):
    return jax.nn.gelu(x, approximate=True)

def _silu(x):
    return jax.nn.silu(x)

def _sigmoid(x):
    return jax.nn.sigmoid(x)

def _layernorm(x, axis=-1, eps=1e-05):
    m = jnp.mean(x, axis=axis, keepdims=True)
    v = jnp.var(x, axis=axis, keepdims=True)
    return (x - m) / jnp.sqrt(v + eps)

def _scatter_add(tgt, idx, src, axis=0):
    return tgt.at[idx].add(src)

def _segment_sum(src, seg, n):
    return jax.ops.segment_sum(src, seg, n)
kernel_name = 'mk_adaln_d2_jaxref_r8_ab0408'

def setup_inputs(seed: int=0):
    np.random.seed(seed)
    _w = jnp.asarray

    def _L0_attn_setup():
        import jax, jax.numpy as jnp
        import numpy as np
        B, L, D = (2, 256, 128)
        H, K = (16, 16)
        HD = D // H

        def tisa_bias(offsets, amplitudes, sharpness, seq_len):
            rel = jnp.arange(-(seq_len - 1), seq_len, dtype=jnp.float32)
            diff = offsets[:, :, None] - rel[None, None, :]
            scores = jnp.sum(amplitudes[:, :, None] * jnp.exp(-jnp.abs(sharpness)[:, :, None] * diff * diff), axis=1)
            i = jnp.arange(seq_len)
            idx = i[:, None] - i[None, :] + (seq_len - 1)
            return scores[:, idx]
        key = jax.random.key(seed)
        k1, k2, k3, k4, k5 = jax.random.split(key, 5)
        x = jax.random.normal(k1, (B, L, D), dtype=jnp.float32)
        w_in = jax.random.normal(k2, (3 * D, D), dtype=jnp.float32) * 0.02
        kernel_offsets = jax.random.normal(k3, (H, K), dtype=jnp.float32) * 20.0
        kernel_amplitudes = 0.1 + 0.01 * jax.random.normal(k4, (H, K), dtype=jnp.float32)
        kernel_sharpness = 0.1 + 0.01 * jax.random.normal(k5, (H, K), dtype=jnp.float32)
        return {'x': x, 'w_in': w_in, 'kernel_offsets': kernel_offsets, 'kernel_amplitudes': kernel_amplitudes, 'kernel_sharpness': kernel_sharpness}
    _L0_attn_in = _L0_attn_setup()

    def _L0_ffn_setup():
        import jax, jax.numpy as jnp
        import numpy as np
        N_EXPERTS = 8
        CAP_FACTOR = 1.25
        BATCH, SEQ, DMODEL, DFF = (4, 256, 128, 512)
        key = jax.random.key(seed)
        k0, k1, k2, k3 = jax.random.split(key, 4)
        x = jax.random.normal(k0, (BATCH, SEQ, DMODEL), dtype=jnp.float32)
        Wr = jax.random.normal(k1, (DMODEL, N_EXPERTS), dtype=jnp.float32) * 0.02
        W1 = jax.random.normal(k2, (N_EXPERTS, DMODEL, DFF), dtype=jnp.float32) * 0.02
        W2 = jax.random.normal(k3, (N_EXPERTS, DFF, DMODEL), dtype=jnp.float32) * 0.02
        return {'x': x, 'Wr': Wr, 'W1': W1, 'W2': W2}
    _L0_ffn_in = _L0_ffn_setup()
    _L0_c = _w((lambda *s: np.random.randn(*s).astype(np.float32) * 0.05)(8, 128))
    _L0_wmod = _w((lambda *s: np.random.randn(*s).astype(np.float32) * 0.05)(128, 6 * 128) * 128 ** (-0.5))

    def _L1_attn_setup():
        import jax, jax.numpy as jnp
        import numpy as np
        B, T, D = (2, 256, 128)
        HV, HK = (16, 8)
        DK, DV = (64, 64)
        K_DIM = HK * DK
        V_DIM = HV * DV
        CONV_DIM = 2 * K_DIM + V_DIM
        KS = 4
        EPS = 1e-06

        def _causal_conv_silu(x, w):
            xp = jnp.pad(x, ((0, 0), (KS - 1, 0), (0, 0)))
            y = sum((xp[:, i:i + x.shape[1], :] * w[:, i] for i in range(KS)))
            return jax.nn.silu(y)

        def _l2norm(x):
            return x * jax.lax.rsqrt(jnp.sum(x * x, -1, keepdims=True) + EPS)

        def _forward(hidden_states, W_qkv, W_z, W_b, W_a, dt_bias, A_log, conv_w, norm_w, W_out):
            b_, t_ = hidden_states.shape[:2]
            mixed_qkv = hidden_states @ W_qkv
            z = (hidden_states @ W_z).reshape(b_, t_, HV, DV)
            beta = jax.nn.sigmoid(hidden_states @ W_b)
            g = -jnp.exp(A_log) * jax.nn.softplus(hidden_states @ W_a + dt_bias)
            mixed_qkv = _causal_conv_silu(mixed_qkv, conv_w)
            q, k, v = jnp.split(mixed_qkv, [K_DIM, 2 * K_DIM], axis=-1)
            q = q.reshape(b_, t_, HK, DK)
            k = k.reshape(b_, t_, HK, DK)
            v = v.reshape(b_, t_, HV, DV)
            rep = HV // HK
            q = jnp.repeat(q, rep, axis=2)
            k = jnp.repeat(k, rep, axis=2)
            q = _l2norm(q) * DK ** (-0.5)
            k = _l2norm(k)
            qT = q.transpose(1, 0, 2, 3)
            kT = k.transpose(1, 0, 2, 3)
            vT = v.transpose(1, 0, 2, 3)
            gT = g.transpose(1, 0, 2)
            bT = beta.transpose(1, 0, 2)

            def step(S, xs):
                q_t, k_t, v_t, g_t, b_t = xs
                S = S * jnp.exp(g_t)[..., None, None]
                kv = jnp.einsum('bhk,bhkv->bhv', k_t, S)
                S = S + jnp.einsum('bhk,bhv->bhkv', k_t, (v_t - kv) * b_t[..., None])
                o_t = jnp.einsum('bhk,bhkv->bhv', q_t, S)
                return (S, o_t)
            S0 = jnp.zeros((b_, HV, DK, DV), jnp.float32)
            _, oT = jax.lax.scan(step, S0, (qT, kT, vT, gT, bT))
            o = oT.transpose(1, 0, 2, 3)
            var = jnp.mean(o * o, axis=-1, keepdims=True)
            o = o * jax.lax.rsqrt(var + EPS) * norm_w * jax.nn.silu(z)
            return o.reshape(b_, t_, V_DIM) @ W_out
        key = jax.random.key(seed)
        ks = jax.random.split(key, 9)
        g = lambda k, shape, sc: jax.random.normal(k, shape, jnp.float32) * sc
        return {'hidden_states': g(ks[0], (B, T, D), 1.0), 'W_qkv': g(ks[1], (D, CONV_DIM), 0.02), 'W_z': g(ks[2], (D, V_DIM), 0.02), 'W_b': g(ks[3], (D, HV), 0.02), 'W_a': g(ks[4], (D, HV), 0.02), 'dt_bias': jnp.ones((HV,), jnp.float32), 'A_log': jnp.log(jax.random.uniform(ks[5], (HV,), jnp.float32, 0.001, 16.0)), 'conv_w': g(ks[6], (CONV_DIM, KS), 0.2), 'norm_w': jnp.ones((DV,), jnp.float32), 'W_out': g(ks[7], (V_DIM, D), 0.02)}
    _L1_attn_in = _L1_attn_setup()

    def _L1_ffn_setup():
        import jax, jax.numpy as jnp
        import numpy as np
        import math
        E = 16
        TOP_K = 2
        D = 128
        F = 512
        SH = 256
        key = jax.random.key(seed)
        ks = jax.random.split(key, 10)
        s = lambda k, shape, fan: jax.random.normal(k, shape, jnp.float32) / np.sqrt(fan)
        return {'x': jax.random.normal(ks[0], (32, 32, D), jnp.float32), 'gate_w': s(ks[1], (E, D), D), 'up_w': s(ks[2], (E, F, D), D), 'up_b': s(ks[3], (E, F), D), 'gw': s(ks[4], (E, F, D), D), 'gb': s(ks[5], (E, F), D), 'down_w': s(ks[6], (E, D, F), F), 'down_b': s(ks[7], (E, D), F), 'sh_gate_w': s(ks[8], (SH, D), D), 'sh_up_w': s(ks[9], (SH, D), D), 'sh_down_w': s(jax.random.fold_in(key, 11), (D, SH), SH)}
    _L1_ffn_in = _L1_ffn_setup()
    _L1_c = _w((lambda *s: np.random.randn(*s).astype(np.float32) * 0.05)(8, 128))
    _L1_wmod = _w((lambda *s: np.random.randn(*s).astype(np.float32) * 0.05)(128, 6 * 128) * 128 ** (-0.5))
    _d = {'L0_attn_x': _L0_attn_in['x'], 'L0_attn_w_in': _L0_attn_in['w_in'], 'L0_attn_kernel_offsets': _L0_attn_in['kernel_offsets'], 'L0_attn_kernel_amplitudes': _L0_attn_in['kernel_amplitudes'], 'L0_attn_kernel_sharpness': _L0_attn_in['kernel_sharpness'], 'L0_ffn_Wr': _L0_ffn_in['Wr'], 'L0_ffn_W1': _L0_ffn_in['W1'], 'L0_ffn_W2': _L0_ffn_in['W2'], 'L0_c': _L0_c, 'L0_wmod': _L0_wmod, 'L1_attn_W_qkv': _L1_attn_in['W_qkv'], 'L1_attn_W_z': _L1_attn_in['W_z'], 'L1_attn_W_b': _L1_attn_in['W_b'], 'L1_attn_W_a': _L1_attn_in['W_a'], 'L1_attn_dt_bias': _L1_attn_in['dt_bias'], 'L1_attn_A_log': _L1_attn_in['A_log'], 'L1_attn_conv_w': _L1_attn_in['conv_w'], 'L1_attn_norm_w': _L1_attn_in['norm_w'], 'L1_attn_W_out': _L1_attn_in['W_out'], 'L1_ffn_gate_w': _L1_ffn_in['gate_w'], 'L1_ffn_up_w': _L1_ffn_in['up_w'], 'L1_ffn_up_b': _L1_ffn_in['up_b'], 'L1_ffn_gw': _L1_ffn_in['gw'], 'L1_ffn_gb': _L1_ffn_in['gb'], 'L1_ffn_down_w': _L1_ffn_in['down_w'], 'L1_ffn_down_b': _L1_ffn_in['down_b'], 'L1_ffn_sh_gate_w': _L1_ffn_in['sh_gate_w'], 'L1_ffn_sh_up_w': _L1_ffn_in['sh_up_w'], 'L1_ffn_sh_down_w': _L1_ffn_in['sh_down_w'], 'L1_c': _L1_c, 'L1_wmod': _L1_wmod}
    _x0 = _d['L0_attn_x']
    _d['L0_attn_x'] = jax.random.normal(jax.random.fold_in(jax.random.key(seed), 1), (8, 512, 128), dtype=_x0.dtype)
    del _x0
    return _d

def reference(L0_attn_x, L0_attn_w_in, L0_attn_kernel_offsets, L0_attn_kernel_amplitudes, L0_attn_kernel_sharpness, L0_ffn_Wr, L0_ffn_W1, L0_ffn_W2, L0_c, L0_wmod, L1_attn_W_qkv, L1_attn_W_z, L1_attn_W_b, L1_attn_W_a, L1_attn_dt_bias, L1_attn_A_log, L1_attn_conv_w, L1_attn_norm_w, L1_attn_W_out, L1_ffn_gate_w, L1_ffn_up_w, L1_ffn_up_b, L1_ffn_gw, L1_ffn_gb, L1_ffn_down_w, L1_ffn_down_b, L1_ffn_sh_gate_w, L1_ffn_sh_up_w, L1_ffn_sh_down_w, L1_c, L1_wmod):

    def _L0_attn_ref(x, w_in, kernel_offsets, kernel_amplitudes, kernel_sharpness):
        import jax, jax.numpy as jnp
        import numpy as np
        B, L, D = (2, 256, 128)
        H, K = (16, 16)
        HD = D // H

        def tisa_bias(offsets, amplitudes, sharpness, seq_len):
            rel = jnp.arange(-(seq_len - 1), seq_len, dtype=jnp.float32)
            diff = offsets[:, :, None] - rel[None, None, :]
            scores = jnp.sum(amplitudes[:, :, None] * jnp.exp(-jnp.abs(sharpness)[:, :, None] * diff * diff), axis=1)
            i = jnp.arange(seq_len)
            idx = i[:, None] - i[None, :] + (seq_len - 1)
            return scores[:, idx]
        b, l, d = x.shape
        proj = jnp.einsum('bld,ed->ble', x, w_in)
        k_, v_, q_ = (proj[..., :d], proj[..., d:2 * d], proj[..., 2 * d:])

        def heads(t):
            return t.reshape(b, l, H, HD).transpose(0, 2, 1, 3)
        q, k, v = (heads(q_), heads(k_), heads(v_))
        bias = tisa_bias(kernel_offsets, kernel_amplitudes, kernel_sharpness, l)
        scale = 1.0 / np.sqrt(HD).astype(np.float32)
        logits = jnp.einsum('bhld,bhmd->bhlm', q, k) * scale + bias[None]
        attn = jax.nn.softmax(logits, axis=-1)
        out = jnp.einsum('bhlm,bhmd->bhld', attn, v)
        return out.transpose(0, 2, 1, 3).reshape(b, l, d)

    def _L0_ffn_ref(x, Wr, W1, W2):
        import jax, jax.numpy as jnp
        import numpy as np
        N_EXPERTS = 8
        CAP_FACTOR = 1.25
        BATCH, SEQ, DMODEL, DFF = (4, 256, 128, 512)
        B, S, D = x.shape
        E = W1.shape[0]
        cap = int(CAP_FACTOR * B * S / E)
        t = x.reshape(-1, D)
        probs = jax.nn.softmax(t @ Wr, axis=-1)
        idx = jnp.argmax(probs, axis=-1)
        pmax = jnp.max(probs, axis=-1)
        onehot = jax.nn.one_hot(idx, E, dtype=jnp.int32)
        pos = jnp.sum(jnp.cumsum(onehot, axis=0) * onehot, axis=-1) - 1
        kept = pos < cap
        flat = idx * cap + jnp.minimum(pos, cap - 1)
        disp = jnp.zeros((E * cap, D), t.dtype).at[flat].add(t * kept[:, None].astype(t.dtype))
        ein = disp.reshape(E, cap, D)
        h = jax.nn.relu(jnp.einsum('ecd,edf->ecf', ein, W1))
        eout = jnp.einsum('ecf,efd->ecd', h, W2).reshape(E * cap, D)
        comb = jnp.where(kept[:, None], eout[flat], t)
        factor = jnp.where(kept, pmax, jnp.ones_like(pmax))
        out = (comb * factor[:, None]).reshape(B, S, D)
        return out

    def _L1_attn_ref(hidden_states, W_qkv, W_z, W_b, W_a, dt_bias, A_log, conv_w, norm_w, W_out):
        import jax, jax.numpy as jnp
        import numpy as np
        B, T, D = (2, 256, 128)
        HV, HK = (16, 8)
        DK, DV = (64, 64)
        K_DIM = HK * DK
        V_DIM = HV * DV
        CONV_DIM = 2 * K_DIM + V_DIM
        KS = 4
        EPS = 1e-06

        def _causal_conv_silu(x, w):
            xp = jnp.pad(x, ((0, 0), (KS - 1, 0), (0, 0)))
            y = sum((xp[:, i:i + x.shape[1], :] * w[:, i] for i in range(KS)))
            return jax.nn.silu(y)

        def _l2norm(x):
            return x * jax.lax.rsqrt(jnp.sum(x * x, -1, keepdims=True) + EPS)

        def _forward(hidden_states, W_qkv, W_z, W_b, W_a, dt_bias, A_log, conv_w, norm_w, W_out):
            b_, t_ = hidden_states.shape[:2]
            mixed_qkv = hidden_states @ W_qkv
            z = (hidden_states @ W_z).reshape(b_, t_, HV, DV)
            beta = jax.nn.sigmoid(hidden_states @ W_b)
            g = -jnp.exp(A_log) * jax.nn.softplus(hidden_states @ W_a + dt_bias)
            mixed_qkv = _causal_conv_silu(mixed_qkv, conv_w)
            q, k, v = jnp.split(mixed_qkv, [K_DIM, 2 * K_DIM], axis=-1)
            q = q.reshape(b_, t_, HK, DK)
            k = k.reshape(b_, t_, HK, DK)
            v = v.reshape(b_, t_, HV, DV)
            rep = HV // HK
            q = jnp.repeat(q, rep, axis=2)
            k = jnp.repeat(k, rep, axis=2)
            q = _l2norm(q) * DK ** (-0.5)
            k = _l2norm(k)
            qT = q.transpose(1, 0, 2, 3)
            kT = k.transpose(1, 0, 2, 3)
            vT = v.transpose(1, 0, 2, 3)
            gT = g.transpose(1, 0, 2)
            bT = beta.transpose(1, 0, 2)

            def step(S, xs):
                q_t, k_t, v_t, g_t, b_t = xs
                S = S * jnp.exp(g_t)[..., None, None]
                kv = jnp.einsum('bhk,bhkv->bhv', k_t, S)
                S = S + jnp.einsum('bhk,bhv->bhkv', k_t, (v_t - kv) * b_t[..., None])
                o_t = jnp.einsum('bhk,bhkv->bhv', q_t, S)
                return (S, o_t)
            S0 = jnp.zeros((b_, HV, DK, DV), jnp.float32)
            _, oT = jax.lax.scan(step, S0, (qT, kT, vT, gT, bT))
            o = oT.transpose(1, 0, 2, 3)
            var = jnp.mean(o * o, axis=-1, keepdims=True)
            o = o * jax.lax.rsqrt(var + EPS) * norm_w * jax.nn.silu(z)
            return o.reshape(b_, t_, V_DIM) @ W_out
        return _forward(hidden_states, W_qkv, W_z, W_b, W_a, dt_bias, A_log, conv_w, norm_w, W_out)

    def _L1_ffn_ref(x, gate_w, up_w, up_b, gw, gb, down_w, down_b, sh_gate_w, sh_up_w, sh_down_w):
        import jax, jax.numpy as jnp
        import numpy as np
        import math
        E = 16
        TOP_K = 2
        D = 128
        F = 512
        SH = 256
        B, S, Dm = x.shape
        h = x.reshape(-1, Dm)
        T = h.shape[0]
        scores = jax.nn.sigmoid(h @ gate_w.T)
        cap = math.ceil(T / E * TOP_K)
        topk_score, topk_ids = jax.lax.top_k(scores.T, cap)
        xin = h[topk_ids]
        up = jnp.einsum('ecd,efd->ecf', xin, up_w) + up_b[:, None, :]
        g = jnp.einsum('ecd,efd->ecf', xin, gw) + gb[:, None, :]
        eo = jax.nn.silu(g) * up
        eo = jnp.einsum('ecf,edf->ecd', eo, down_w) + down_b[:, None, :]
        flat = (eo * topk_score[..., None]).reshape(-1, Dm)
        out = jnp.zeros_like(h).at[topk_ids.reshape(-1)].add(flat)
        out = out.reshape(B, S, Dm)
        shared = jax.nn.silu(jnp.einsum('bsd,fd->bsf', x, sh_gate_w)) * jnp.einsum('bsd,fd->bsf', x, sh_up_w)
        shared = jnp.einsum('bsf,df->bsd', shared, sh_down_w)
        return out + shared
    x = L0_attn_x
    mod = (_silu(L0_c) @ L0_wmod).reshape(L0_c.shape[0], 6, 1, -1)
    sa, ca, ga, sb, cb, gb = (mod[:, 0], mod[:, 1], mod[:, 2], mod[:, 3], mod[:, 4], mod[:, 5])
    ga = (2 * (ga >= 0) - 1) * jnp.maximum(jnp.abs(ga), 0.25)
    gb = (2 * (gb >= 0) - 1) * jnp.maximum(jnp.abs(gb), 0.25)
    h = _layernorm(x, axis=-1) * (1 + ca) + sa
    x = x + ga * _L0_attn_ref(h, L0_attn_w_in, L0_attn_kernel_offsets, L0_attn_kernel_amplitudes, L0_attn_kernel_sharpness)
    h = _layernorm(x, axis=-1) * (1 + cb) + sb
    x = x + gb * _L0_ffn_ref(h, L0_ffn_Wr, L0_ffn_W1, L0_ffn_W2)
    mod = (_silu(L1_c) @ L1_wmod).reshape(L1_c.shape[0], 6, 1, -1)
    sa, ca, ga, sb, cb, gb = (mod[:, 0], mod[:, 1], mod[:, 2], mod[:, 3], mod[:, 4], mod[:, 5])
    ga = (2 * (ga >= 0) - 1) * jnp.maximum(jnp.abs(ga), 0.25)
    gb = (2 * (gb >= 0) - 1) * jnp.maximum(jnp.abs(gb), 0.25)
    h = _layernorm(x, axis=-1) * (1 + ca) + sa
    x = x + ga * _L1_attn_ref(h, L1_attn_W_qkv, L1_attn_W_z, L1_attn_W_b, L1_attn_W_a, L1_attn_dt_bias, L1_attn_A_log, L1_attn_conv_w, L1_attn_norm_w, L1_attn_W_out)
    h = _layernorm(x, axis=-1) * (1 + cb) + sb
    x = x + gb * _L1_ffn_ref(h, L1_ffn_gate_w, L1_ffn_up_w, L1_ffn_up_b, L1_ffn_gw, L1_ffn_gb, L1_ffn_down_w, L1_ffn_down_b, L1_ffn_sh_gate_w, L1_ffn_sh_up_w, L1_ffn_sh_down_w)
    return x

_drawn_inputs = setup_inputs


def setup_inputs(seed=0):
    import zlib

    import numpy as np

    out = dict(_drawn_inputs(seed))
    spreads = {'L1_attn_dt_bias': (1.0, 0.6), 'L1_attn_norm_w': (1.0, 0.6)}
    factors = {'L0_attn_w_in': 6.503,
     'L0_attn_kernel_offsets': 8.0,
     'L0_attn_kernel_amplitudes': 41.418,
     'L0_attn_kernel_sharpness': 61.993,
     'L0_ffn_Wr': 6.434,
     'L0_ffn_W1': 6.463,
     'L0_ffn_W2': 5.655,
     'L0_c': 4.944,
     'L0_wmod': 5.197,
     'L1_attn_W_qkv': 3.937,
     'L1_attn_W_z': 3.87,
     'L1_attn_W_b': 8.0,
     'L1_attn_W_a': 23.283,
     'L1_attn_A_log': 7.905,
     'L1_attn_conv_w': 4.217,
     'L1_attn_W_out': 4.646,
     'L1_ffn_up_b': 3.674,
     'L1_ffn_gb': 3.569,
     'L1_ffn_down_b': 4.443}
    for name, (base, spread) in spreads.items():
        noise = np.random.default_rng([zlib.crc32(name.encode()), seed]).standard_normal(out[name].shape)
        drawn = base * np.exp(spread * noise) if base else spread * noise
        out[name] = jnp.asarray(drawn.astype(out[name].dtype))
    for name, factor in factors.items():
        out[name] = (out[name] * factor).astype(out[name].dtype)
    return out
```

```python
import concourse.bass as bass
from concourse import mybir
from contextlib import ExitStack

F32 = mybir.dt.float32
BF16 = mybir.dt.bfloat16
I32 = mybir.dt.int32
ALU = mybir.AluOpType
ACT = mybir.ActivationFunctionType
AX = mybir.AxisListType

B, L, D = 8, 512, 128
P = 128
LT = L // P
NT = B * LT
LN_EPS = 1e-5
GA, SB, CB, GB = range(4)

H0, K0 = 16, 16
HD0 = D // H0
HG = 4
BW = L + 3 * P

E0, F0 = 8, 512
CAP0 = int(1.25 * B * L / E0)
SLOTS0 = E0 * CAP0

HV, HK, DK = 16, 8, 64
KD, VD = HK * DK, HV * DK
CD = 2 * KD + VD
KS = 4
EPS1 = 1e-6

E1, F1, SH = 16, 512, 256
CAP1 = 2 * B * L // E1


def bcast(ap, axis, n):
    a = [list(x) for x in ap.ap]
    a.insert(axis, [0, n])
    return bass.AP(ap.tensor, ap.offset, a)


def reversed_tiles(ap):
    part, (step, n) = [list(x) for x in ap.ap]
    return bass.AP(ap.tensor, ap.offset + (P - 1) * step, [part, [P * step, n // P], [-step, P]])


class Stage:

    top = 0

    def __init__(self, nc, names):
        self.nc, self.ctx = nc, ExitStack()
        self.sems = {n: self.ctx.enter_context(nc.semaphore(n, num=Stage.top + i)) for i, n in enumerate(names)}
        self.range = range(Stage.top, Stage.top + len(self.sems))
        Stage.top = self.range.stop

    def __getitem__(self, name):
        return self.sems[name]

    def __enter__(self):
        return self

    def __exit__(self, *a):
        self.ctx.close()
        Stage.top = self.range.start

    def sb(self, name, shape, dt=F32):
        return self.ctx.enter_context(self.nc.sbuf_tensor(name, shape, dt, allow_name_mangling=True))

    def end(self, pool_dmas=False):
        if pool_dmas:
            self.nc.gpsimd.dma_reset(self.range)
        self.nc.all_engine_barrier(sems_to_clear=self.range)


def linker(eng, sem):
    count = [0]

    def link(ins):
        count[0] += 1
        ins.then_inc(sem, 1)
        eng.wait_ge(sem, count[0])
    return link


def layer_norm(nc, dve, link, x, stats, mv, rstd, out, tiles, var_ready, rstd_ready):
    for i in range(tiles):
        last = nc.vector.bn_stats(stats[:, i, :], x(i))
    link(last)
    for i in range(tiles):
        last = nc.vector.bn_aggr(mv[:, i, :], stats[:, i, :])
    link(last)
    nc.vector.tensor_scalar(rstd[:, 0:tiles], mv[:, 0:tiles, 1], LN_EPS, None, ALU.add).then_inc(var_ready, 1)
    dve.wait_ge(rstd_ready, 1)
    link(nc.vector.reciprocal(rstd[:, 0:tiles], rstd[:, 0:tiles]))
    for i in range(tiles):
        last = nc.vector.tensor_scalar(out(i), x(i), mv[:, i, 0:1], rstd[:, i:i + 1],
                                       ALU.subtract, ALU.mult)
    return last


def root(nc, act, rstd, var_ready, rstd_ready):
    act.wait_ge(var_ready, 1)
    nc.scalar.activation(rstd, rstd, ACT.Sqrt).then_inc(rstd_ready, 1)


def setup(nc, g, a):
    with Stage(nc, ["s_load", "s_id", "s_silu", "s_cT", "s_cTs", "s_mc", "s_dve", "s_pool", "s_zero",
                    "s_disp"]) as s:
        c_sb = s.sb("c_sb", [B, 2, D])
        sc_sb = s.sb("sc_sb", [B, 2, D])
        wmod = s.sb("wmod", [D, 2, 6 * D])
        zero = s.sb("zero", [P, SLOTS0 // P * D])
        PB, cT = g["PB"], g["cT"]
        with nc.Block() as block:
            @block.sync
            def _(sp):
                sp.dma_start(c_sb[:, 0, :], a["L0_c"]).then_inc(s["s_load"], 16)
                sp.dma_start(c_sb[:, 1, :], a["L1_c"]).then_inc(s["s_load"], 16)
                sp.dma_start(wmod[:, 0, :], a["L0_wmod"]).then_inc(s["s_load"], 16)
                sp.dma_start(wmod[:, 1, :], a["L1_wmod"]).then_inc(s["s_load"], 16)
                sp.dma_start(g["X"][:, :, :], a["L0_attn_x"].rearrange("b (t p) d -> p (b t) d", p=P))\
                  .then_inc(s["s_load"], 16)
                sp.wait_ge(s["s_zero"], 1)
                sp.dma_start(g["disp"].rearrange("(p r) d -> p (r d)", p=P), zero[:, :]).then_inc(s["s_disp"], 16)
                sp.wait_ge(s["s_load"], 80)
                sp.wait_ge(s["s_disp"], 16)

            @block.gpsimd
            def _(pool):
                nc.gpsimd.memset(g["ident"][:, :], 0.0).then_inc(s["s_pool"], 1)
                nc.gpsimd.memset(g["ones"][:, :], 1.0).then_inc(s["s_pool"], 1)
                nc.gpsimd.memset(zero[:, :], 0.0).then_inc(s["s_zero"], 1)
                pool.wait_ge(s["s_pool"], 2)
                nc.gpsimd.affine_select(out=g["ident"][:, :], in_=g["ident"][:, :], compare_op=ALU.not_equal,
                                        fill=1.0, base=0, pattern=[[-1, P]], channel_multiplier=1)\
                    .then_inc(s["s_id"], 1)
                nc.gpsimd.affine_select(out=g["tri"][:, :], in_=g["ones"][:, :], compare_op=ALU.is_ge,
                                        fill=0.0, base=0, pattern=[[1, P]], channel_multiplier=-1)\
                    .then_inc(s["s_pool"], 1)
                pool.wait_ge(s["s_pool"], 3)

            @block.scalar
            def _(act):
                act.wait_ge(s["s_load"], 80)
                nc.scalar.activation(sc_sb[:, :, :], c_sb[:, :, :], ACT.Silu).then_inc(s["s_silu"], 1)

            @block.tensor
            def _(pe):
                pe.wait_ge(s["s_id"], 1)
                pe.wait_ge(s["s_silu"], 1)
                for l in range(2):
                    last = nc.tensor.transpose(PB[0][:, l * B:(l + 1) * B], sc_sb[:, l, :],
                                               g["ident"][0:B, 0:B])
                last.then_inc(s["s_cT"], 1)
                pe.wait_ge(s["s_cTs"], 1)
                for l in range(2):
                    for j in range(6):
                        at = (l * 6 + j) * B
                        last = nc.tensor.matmul(PB[1][:, at:at + B], wmod[:, l, j * D:(j + 1) * D],
                                                cT[:, l, :], start=True, stop=True)
                last.then_inc(s["s_mc"], 1)

            @block.vector
            def _(dve):
                link = linker(dve, s["s_dve"])
                dve.wait_ge(s["s_cT"], 1)
                nc.vector.tensor_copy(cT[:, :, :], PB[0][:, 0:2 * B].rearrange("p (l b) -> p l b", l=2))\
                    .then_inc(s["s_cTs"], 1)
                dve.wait_ge(s["s_mc"], 1)
                link(nc.vector.tensor_copy(g["MODC"][:, :, :, :],
                                           PB[1][:, 0:12 * B].rearrange("p (l j b) -> p l j b", l=2, j=6)))
                link(nc.vector.tensor_scalar(g["MODC"][:, :, 1, :], g["MODC"][:, :, 1, :], 1.0, None, ALU.add))
        s.end()


def modulate(nc, g, a, layer):
    PB, MB = g["PB"], g["MODB"]
    with Stage(nc, ["m_load", "m_cTb", "m_mb", "m_out", "m_dve"]) as s:
        cTb = s.sb("cTb", [D, B, P])
        wmod = s.sb("wmod1", [D, 4 * D])
        sgn = s.sb("sgn", [P, B, P])
        mag = s.sb("mag", [P, B, P])
        with nc.Block() as block:
            @block.sync
            def _(sp):
                sp.dma_start(wmod[:, :], a[f"L{layer}_wmod"][:, 2 * D:6 * D]).then_inc(s["m_load"], 16)

            @block.tensor
            def _(pe):
                pe.wait_ge(s["m_load"], 16)
                pe.wait_ge(s["m_cTb"], 1)
                for b in range(B):
                    nc.tensor.matmul(PB[b][:, :], cTb[:, b, :], wmod[:, :], start=True, stop=True)\
                        .then_inc(s["m_mb"], 1)

            @block.scalar
            def _(act):
                for b in range(B):
                    act.wait_ge(s["m_mb"], b + 1)
                    nc.scalar.activation(MB[:, b, :, :], PB[b][:, :].rearrange("p (j d) -> p j d", j=4), ACT.Copy)\
                        .then_inc(s["m_out"], 1)

            @block.vector
            def _(dve):
                link = linker(dve, s["m_dve"])
                nc.vector.tensor_copy(cTb[:, :, :], bcast(g["cT"][:, layer, :], 2, P)).then_inc(s["m_cTb"], 1)
                dve.wait_ge(s["m_out"], B)
                link(nc.vector.tensor_scalar(MB[:, :, CB, :], MB[:, :, CB, :], 1.0, None, ALU.add))
                for j in (GA, GB):
                    link(nc.vector.tensor_scalar(sgn[:, :, :], MB[:, :, j, :], 0.0, 2.0, ALU.is_ge, ALU.mult))
                    link(nc.vector.scalar_tensor_tensor(mag[:, :, :], sgn[:, :, :], -1.0, MB[:, :, j, :],
                                                        ALU.add, ALU.mult))
                    link(nc.vector.tensor_scalar(mag[:, :, :], mag[:, :, :], 0.25, None, ALU.max))
                    link(nc.vector.scalar_tensor_tensor(MB[:, :, j, :], sgn[:, :, :], -1.0, mag[:, :, :],
                                                        ALU.add, ALU.mult))
        s.end()


def attention0(nc, g, a):
    SCALE = float(1.0 / HD0 ** 0.5)
    PB, X, ident = g["PB"], g["X"], g["ident"]
    NG = H0 // HG
    with Stage(nc, ["a_load", "a_w", "a_wT", "a_wp", "a_dve", "a_io", "a_ex", "a_amp", "a_sc", "a_sce",
                    "a_scd", "a_bias", "a_init"]) as s:
        wq = s.sb("wq", [D, NG, HG, 32])
        wk = s.sb("wk", [D, NG, HG, 32])
        wv = s.sb("wv", [D, D])
        Tb = s.sb("Tb", [P, H0, BW])
        qp = s.sb("qp", [P, NG, L])
        kz = s.sb("kz", [P, H0, L])
        vp = s.sb("vp", [P, LT, H0, 32])
        with ExitStack() as tmp:
            wl = tmp.enter_context(nc.sbuf_tensor("wl", [P, 3, D], F32))
            par = tmp.enter_context(nc.sbuf_tensor("par", [P, 2, 3], F32))
            neg = tmp.enter_context(nc.sbuf_tensor("neg", [P, 2], F32))
            rel = tmp.enter_context(nc.sbuf_tensor("rel", [P, 1024], F32))
            dif = tmp.enter_context(nc.sbuf_tensor("dif", [P, 2, 1024], F32))
            dif2 = tmp.enter_context(nc.sbuf_tensor("dif2", [P, 2, 1024], F32))
            blk = tmp.enter_context(nc.sbuf_tensor("blk", [P, 8], F32))
            amp = tmp.enter_context(nc.sbuf_tensor("amp", [P, 2, 8], F32))
            sc = tmp.enter_context(nc.sbuf_tensor("sc", [8, 2, 1024], F32))
            with nc.Block() as block:
                @block.sync
                def _(sp):
                    sp.dma_start(wl[:, :, :], a["L0_attn_w_in"].rearrange("(t e) d -> e t d", e=P))\
                      .then_inc(s["a_load"], 16)
                    for j, n in enumerate(("offsets", "amplitudes", "sharpness")):
                        v = a[f"L0_attn_kernel_{n}"].rearrange("(t h) k -> (h k) t", t=2)
                        with nc.allow_non_contiguous_dma(reason="256 parameters, once"):
                            sp.dma_start(par[:, :, j], v).then_inc(s["a_load"], 16)
                    sp.wait_ge(s["a_sce"], 4)
                    sp.dma_start(g["scores"].rearrange("(t h) z -> h t z", t=2), sc[:, :, :])\
                      .then_inc(s["a_scd"], 16)
                    sp.wait_ge(s["a_scd"], 16)
                    sp.dma_start(Tb[:, :, :], bass.AP(g["scores"].tensor, 0, [[1, P], [1024, H0], [1, BW]]))\
                      .then_inc(s["a_bias"], 16)
                    sp.wait_ge(s["a_bias"], 16)

                @block.gpsimd
                def _(pool):
                    nc.gpsimd.iota(rel[:, :], pattern=[[-1, 1024]], base=L - 1, channel_multiplier=0,
                                   allow_small_or_imprecise_dtypes=True).then_inc(s["a_io"], 1)
                    nc.gpsimd.memset(blk[:, :], 1.0).then_inc(s["a_init"], 1)
                    pool.wait_ge(s["a_init"], 1)
                    nc.gpsimd.affine_select(out=blk[:, :], in_=blk[:, :], compare_op=ALU.is_ge, fill=0.0,
                                            base=0, pattern=[[-K0, 8]], channel_multiplier=1)\
                        .then_inc(s["a_init"], 1)
                    pool.wait_ge(s["a_init"], 2)
                    nc.gpsimd.affine_select(out=blk[:, :], in_=blk[:, :], compare_op=ALU.is_ge, fill=0.0,
                                            base=K0 - 1, pattern=[[K0, 8]], channel_multiplier=-1)\
                        .then_inc(s["a_io"], 1)
                    nc.gpsimd.memset(kz[:, :, :], 0.0)
                    nc.gpsimd.memset(wq[:, :, :, :], 0.0).then_inc(s["a_init"], 1)
                    nc.gpsimd.memset(wk[:, :, :, :], 0.0).then_inc(s["a_init"], 1)
                    nc.gpsimd.memset(vp[:, :, :, :], 0.0).then_inc(s["a_init"], 1)
                    pool.wait_ge(s["a_init"], 5)
                    nc.gpsimd.memset(vp[:, :, :, HD0:HD0 + 1], 1.0).then_inc(s["a_init"], 1)

                @block.vector
                def _(dve):
                    link = linker(dve, s["a_dve"])
                    dve.wait_ge(s["a_load"], 64)
                    link(nc.vector.scalar_tensor_tensor(neg[:, :], par[:, :, 2], -1.0, par[:, :, 2],
                                                        ALU.mult, ALU.min))
                    dve.wait_ge(s["a_io"], 2)
                    for t in range(2):
                        nc.vector.tensor_scalar(amp[:, t, :], blk[:, :], par[:, t, 1:2], None, ALU.mult)\
                            .then_inc(s["a_amp"], 1)
                        link(nc.vector.tensor_scalar(dif[:, t, :], rel[:, :], par[:, t, 0:1], None,
                                                     ALU.subtract))
                        link(nc.vector.tensor_scalar(dif2[:, t, :], dif[:, t, :], neg[:, t:t + 1], None,
                                                     ALU.mult))
                        nc.vector.tensor_tensor(dif2[:, t, :], dif2[:, t, :], dif[:, t, :], ALU.mult)\
                            .then_inc(s["a_amp"], 1)
                    dve.wait_ge(s["a_wT"], 1)
                    dve.wait_ge(s["a_init"], 5)
                    w = PB[0][:, 0:3 * D]
                    v4 = lambda t: w[:, t * D:(t + 1) * D].rearrange("p (q h c) -> p q h c", q=NG, h=HG)
                    nc.vector.tensor_copy(wk[:, :, :, 0:HD0], v4(0)).then_inc(s["a_wp"], 1)
                    nc.vector.tensor_copy(wv[:, :], w[:, D:2 * D]).then_inc(s["a_wp"], 1)
                    nc.vector.tensor_copy(wq[:, :, :, 0:HD0], v4(2)).then_inc(s["a_wp"], 1)
                    for n in range(4):
                        dve.wait_ge(s["a_sc"], n + 1)
                        nc.vector.tensor_copy(sc[:, n // 2, (n % 2) * 512:(n % 2 + 1) * 512], PB[4 + n][0:8, :])\
                            .then_inc(s["a_sce"], 1)

                @block.scalar
                def _(act):
                    for t in range(2):
                        act.wait_ge(s["a_amp"], 2 * t + 2)
                        nc.scalar.activation(dif2[:, t, :], dif2[:, t, :], ACT.Exp).then_inc(s["a_ex"], 1)

                @block.tensor
                def _(pe):
                    pe.wait_ge(s["a_load"], 64)
                    for t in range(3):
                        last = nc.tensor.transpose(PB[0][:, t * D:(t + 1) * D], wl[:, t, :], ident[:, :])
                    last.then_inc(s["a_wT"], 1)
                    for n in range(4):
                        pe.wait_ge(s["a_ex"], n // 2 + 1)
                        nc.tensor.matmul(PB[4 + n][0:8, :], amp[:, n // 2, :],
                                         dif2[:, n // 2, (n % 2) * 512:(n % 2 + 1) * 512],
                                         start=True, stop=True).then_inc(s["a_sc"], 1)
            s.end()
        NS, NPT, NPS = 4, 2, 4
        with Stage(nc, ["b_ln", "b_var", "b_rstd", "b_mc", "b_xn", "b_xT", "b_hT", "b_proj", "b_q", "b_k", "b_v", "b_qk",
                        "b_s", "b_exp", "b_pt", "b_evd", "b_eva", "b_pv", "b_oT", "b_o", "b_fin"]) as r:
            st = r.sb("st", [P, LT, 6])
            mv = r.sb("mv", [P, LT, 2])
            rstd = r.sb("rstd", [P, LT])
            xh = r.sb("xh", [P, LT, D])
            mc = r.sb("mc", [P, 6])
            hT = r.sb("hT", [D, L])
            S = r.sb("S", [P, NS, L])
            nmax = r.sb("nmax", [P, NS])
            Pr = r.sb("Pr", [P, 2, LT, L])
            PT = r.sb("PT", [P, NPS, L])
            oT = r.sb("oT", [P, NG, L])
            rec = r.sb("rec", [P, LT, H0])
            o1 = r.sb("o1", [P, LT, D])
            pS, pT, pO = PB[0:2], PB[2:4], PB[4:6]
            pM = PB[6:8]
            NH = H0 * LT
            with nc.Fori(0, B) as b:
                with nc.Block(no_gpsimd_drain=True) as block:
                    @block.vector
                    def _(dve):
                        link = linker(dve, r["b_ln"])
                        nc.vector.tensor_copy(mc[:, :], g["MODC"][:, 0, :, bass.ds(b, 1)]
                                              .rearrange("p j o -> p (j o)")).then_inc(r["b_mc"], 1)
                        layer_norm(nc, dve, link, lambda i: X[:, bass.ds(b * LT + i, 1), :]
                                   .rearrange("p o d -> p (o d)"), st, mv, rstd,
                                   lambda i: xh[:, i, :], LT, r["b_var"], r["b_rstd"]).then_inc(r["b_xn"], 1)
                        for q in range(NG):
                            dve.wait_ge(r["b_proj"], 2 * q + 2)
                            for h in range(HG):
                                last = nc.vector.tensor_copy(kz[32 * h:32 * h + 32, q * HG + h, :],
                                                             pS[1][32 * h:32 * h + 32, :] if q % 2 == 0
                                                             else pM[1][32 * h:32 * h + 32, :])
                            last.then_inc(r["b_k"], 1)
                        dve.wait_ge(r["b_proj"], 2 * NG + 1)
                        nc.vector.tensor_copy(vp[:, :, :, 0:HD0],
                                              pO[0][:, :].rearrange("p (t h c) -> p t h c", t=LT, h=H0))\
                            .then_inc(r["b_v"], 1)

                        def evac(m):
                            dve.wait_ge(r["b_pt"], m + 1)
                            if m >= NPS:
                                dve.wait_ge(r["b_pv"], m - NPS + 1)
                            nc.vector.tensor_copy(PT[:, m % NPS, :], pT[m % NPT][:, :]).then_inc(r["b_evd"], 1)

                        for n in range(NH + LT):
                            h, i = n // LT, n % LT
                            if n < NH:
                                dve.wait_ge(r["b_qk"], n + 1)
                                if n >= NS:
                                    dve.wait_ge(r["b_exp"], n - NS + 1)
                                at = 3 * P - i * P
                                nc.vector.tensor_tensor_reduce(
                                    out=S[:, n % NS, :], in0=pS[n % 2][:, :], in1=Tb[:, h, at:at + L],
                                    scale=-1.0, scalar=3.0e38, op0=ALU.add, op1=ALU.min,
                                    accum_out=nmax[:, n % NS:n % NS + 1]).then_inc(r["b_s"], 1)
                            if h >= 1 and i % 2 == 0:
                                evac(n - LT)
                        link2 = linker(dve, r["b_fin"])
                        for t in range(LT):
                            dve.wait_ge(r["b_o"], t + 1)
                            ob = (pS + pM)[t][:, :].rearrange("p (h c) -> p h c", c=32)
                            link2(nc.vector.reciprocal(rec[:, t, :], ob[:, :, HD0]))
                            link2(nc.vector.tensor_tensor(o1[:, t, :].rearrange("p (h c) -> p h c", c=HD0),
                                                          ob[:, :, 0:HD0], bcast(rec[:, t, :], 2, HD0), ALU.mult))
                            link2(nc.vector.tensor_tensor(o1[:, t, :], o1[:, t, :],
                                                          g["MODB"][:, bass.ds(b, 1), GA, :]
                                                          .rearrange("p o d -> p (o d)"), ALU.mult))
                            xt = X[:, bass.ds(b * LT + t, 1), :].rearrange("p o d -> p (o d)")
                            link2(nc.vector.tensor_tensor(xt, xt, o1[:, t, :], ALU.add))

                    @block.scalar
                    def _(act):
                        root(nc, act, rstd[:, :], r["b_var"], r["b_rstd"])
                        act.wait_ge(r["b_mc"], 1)
                        act.wait_ge(r["b_xT"], 1)
                        nc.scalar.activation(hT[:, :], pM[0][:, :], ACT.Identity, bias=mc[:, 0:1],
                                             scale=mc[:, 1:2]).then_inc(r["b_hT"], 1)
                        for q in range(NG):
                            act.wait_ge(r["b_proj"], 2 * q + 1)
                            nc.scalar.activation(qp[:, q, :].rearrange("p (t i) -> p t i", t=LT),
                                                 reversed_tiles((pS if q % 2 == 0 else pM)[0][:, :]), ACT.Copy,
                                                 scale=SCALE).then_inc(r["b_q"], 1)

                        def evac(m):
                            act.wait_ge(r["b_pt"], m + 1)
                            if m >= NPS:
                                act.wait_ge(r["b_pv"], m - NPS + 1)
                            nc.scalar.activation(PT[:, m % NPS, :], pT[m % NPT][:, :], ACT.Copy)\
                                .then_inc(r["b_eva"], 1)

                        def take(q):
                            act.wait_ge(r["b_pv"], (q + 1) * HG * LT)
                            nc.scalar.activation(oT[:, q, :].rearrange("p (t i) -> p t i", t=LT),
                                                 reversed_tiles(pO[q % 2][:, :]), ACT.Copy).then_inc(r["b_oT"], 1)

                        for n in range(NH + LT):
                            h, i = n // LT, n % LT
                            if n < NH:
                                act.wait_ge(r["b_s"], n + 1)
                                if h >= 2 and i == 0:
                                    act.wait_ge(r["b_pt"], (h - 1) * LT)
                                nc.scalar.activation(Pr[:, h % 2, i, :], S[:, n % NS, :], ACT.Exp, scale=-1.0,
                                                     bias=nmax[:, n % NS:n % NS + 1]).then_inc(r["b_exp"], 1)
                            if h >= 1 and i % 2 == 1:
                                evac(n - LT)
                            if i == LT - 1 and h >= HG + 1 and (h - 1) % HG == 0:
                                take((h - 1) // HG - 1)
                        take(NG - 1)

                    @block.tensor
                    def _(pe):
                        pe.wait_ge(r["b_xn"], 1)
                        for t in range(LT):
                            last = nc.tensor.transpose(pM[0][:, t * P:(t + 1) * P], xh[:, t, :], ident[:, :])
                        last.then_inc(r["b_xT"], 1)
                        pe.wait_ge(r["b_hT"], 1)
                        for q in range(NG):
                            bank = pS if q % 2 == 0 else pM
                            if q >= 2:
                                pe.wait_ge(r["b_q"], q - 1)
                            nc.tensor.matmul(bank[0][:, :], wq[:, q, :, :].rearrange("p h c -> p (h c)"), hT[:, :],
                                             start=True, stop=True).then_inc(r["b_proj"], 1)
                            if q >= 2:
                                pe.wait_ge(r["b_k"], q - 1)
                            nc.tensor.matmul(bank[1][:, :], wk[:, q, :, :].rearrange("p h c -> p (h c)"), hT[:, :],
                                             start=True, stop=True).then_inc(r["b_proj"], 1)
                        for t in range(LT):
                            last = nc.tensor.matmul(pO[0][:, t * P:(t + 1) * P], hT[:, t * P:(t + 1) * P], wv[:, :],
                                                    start=True, stop=True)
                        last.then_inc(r["b_proj"], 1)

                        def scores(n):
                            h, i = n // LT, n % LT
                            if n == 0:
                                pe.wait_ge(r["b_q"], NG)
                                pe.wait_ge(r["b_k"], NG)
                            if n >= 2:
                                pe.wait_ge(r["b_s"], n - 1)
                            nc.tensor.matmul(pS[n % 2][:, :], qp[:, h // HG, i * P:(i + 1) * P], kz[:, h, :],
                                             start=True, stop=True).then_inc(r["b_qk"], 1)

                        def evacuated(m):
                            pe.wait_ge(r["b_evd"] if m % 2 == 0 else r["b_eva"], m // 2 + 1)

                        def transposes(m):
                            h, j = m // LT, m % LT
                            if j == 0:
                                pe.wait_ge(r["b_exp"], LT * (h + 1))
                            if m >= NPT:
                                evacuated(m - NPT)
                            for t in range(LT):
                                last = nc.tensor.transpose(pT[m % NPT][:, t * P:(t + 1) * P],
                                                           Pr[:, h % 2, t, j * P:(j + 1) * P], ident[:, :])
                            last.then_inc(r["b_pt"], 1)

                        def values(m):
                            h, j = m // LT, m % LT
                            evacuated(m)
                            if m == 0:
                                pe.wait_ge(r["b_v"], 1)
                            if j == 0 and h % HG == 0 and h // HG >= 2:
                                pe.wait_ge(r["b_oT"], h // HG - 1)
                            at = 32 * (h % HG)
                            nc.tensor.matmul(pO[h // HG % 2][at:at + 32, :], vp[:, j, h, :], PT[:, m % NPS, :],
                                             start=(j == 0), stop=(j == LT - 1),
                                             tile_position=(0, at)).then_inc(r["b_pv"], 1)

                        for n in range(NH + LT):
                            if n < NH:
                                scores(n)
                            if n >= LT:
                                transposes(n - LT)
                            if n >= LT + 1:
                                values(n - LT - 1)
                        values(NH - 1)
                        pe.wait_ge(r["b_oT"], NG)
                        pe.wait_ge(r["b_s"], NH)
                        for t in range(LT):
                            for q in range(NG):
                                last = nc.tensor.transpose((pS + pM)[t][:, q * P:(q + 1) * P],
                                                           oT[:, q, t * P:(t + 1) * P], ident[:, :])
                            last.then_inc(r["b_o"], 1)
                r.end()


def globals_(nc, ctx):
    with nc.semaphore("first") as first:
        Stage.top = first.num
    sb = lambda n, s, d=F32: ctx.enter_context(nc.sbuf_tensor(n, s, d))
    g = {
        "X": sb("X", [P, NT, D]),
        "MODC": sb("MODC", [P, 2, 6, B]),
        "MODB": sb("MODB", [P, B, 4, D]),
        "cT": sb("cT", [D, 2, B]),
        "ident": sb("ident", [P, P]),
        "ones": sb("ones", [P, P], BF16),
        "tri": sb("tri", [P, P], BF16),
        "PB": [ctx.enter_context(nc.psum_tensor(f"bank{i}", [P, 512], F32)) for i in range(8)],
        "scores": nc.dram_tensor("scores", (H0, 1024), F32).ap(),
        "eout": nc.dram_tensor("eout", (SLOTS0, D), F32).ap(),
        "acc": nc.dram_tensor("acc", (B * L, D), F32).ap(),
        "rows": nc.dram_tensor("rows", (B * L, ROW1), F32).ap(),
        "ids": nc.dram_tensor("slot_ids", (E1 * CAP1,), I32).ap(),
        "disp": nc.dram_tensor("disp", (SLOTS0, D), F32).ap(),
    }
    return g


def store(nc, g, out):
    with Stage(nc, ["z_out"]) as s:
        with nc.Block() as block:
            @block.sync
            def _(sp):
                sp.dma_start(out.rearrange("b (t p) d -> p (b t) d", p=P), g["X"][:, :, :]).then_inc(s["z_out"], 16)
                sp.wait_ge(s["z_out"], 16)
        s.end()


def tokens_of(x, b):
    return x[:, bass.ds(b * LT, LT), :]


def norm_router(nc, g, s, wr, E, shared=None):
    PB, X, H, LG, ident = g["PB"], g["X"], g["H"], g["LG"], g["ident"]
    st = s.sb("st", [P, LT, 6])
    mv = s.sb("mv", [P, LT, 2])
    rstd = s.sb("rstd", [P, LT])
    xh = s.sb("xh", [P, LT, D])
    hT = s.sb("hT", [D, L])
    if shared:
        sg = s.sb("sg", [P, 2, L])
        su = s.sb("su", [P, 2, L])
        so = s.sb("so", [P, LT, D])
    with nc.Fori(0, B) as b:
        with nc.Block(no_gpsimd_drain=True) as block:
            @block.vector
            def _(dve):
                link = linker(dve, s["n_ln"])
                link(layer_norm(nc, dve, link, lambda i: X[:, bass.ds(b * LT + i, 1), :]
                                .rearrange("p o d -> p (o d)"), st, mv, rstd,
                                lambda i: xh[:, i, :], LT, s["n_var"], s["n_rstd"]))
                row = lambda j: bcast(g["MODB"][:, bass.ds(b, 1), j, :], 1, LT)\
                    .rearrange("p t o d -> p t (o d)")
                link(nc.vector.tensor_tensor(xh[:, :, :], xh[:, :, :], row(CB), ALU.mult))
                link(nc.vector.tensor_tensor(xh[:, :, :], xh[:, :, :], row(SB), ALU.add))
                nc.vector.tensor_copy(tokens_of(H, b), xh[:, :, :]).then_inc(s["n_h"], 1)
                dve.wait_ge(s["n_lg"], 1)
                nc.vector.tensor_copy(LG[:, bass.ds(b * LT, LT), 0:E], PB[1][:, 0:LT * E].rearrange("p (t e) -> p t e", t=LT))\
                    .then_inc(s["n_lge"], 1)
                if shared:
                    for c in range(2):
                        dve.wait_ge(s["n_sup"], c + 1)
                        dve.wait_ge(s["n_sg"], c + 1)
                        nc.vector.tensor_tensor(su[:, c, :], PB[4 + c][:, :], sg[:, c, :], ALU.mult)\
                            .then_inc(s["n_su"], 1)
                    dve.wait_ge(s["n_so"], 1)
                    nc.vector.tensor_copy(so[:, :, :], PB[6][:, :].rearrange("p (t d) -> p t d", t=LT))\
                        .then_inc(s["n_soe"], 1)

            @block.scalar
            def _(act):
                root(nc, act, rstd[:, :], s["n_var"], s["n_rstd"])
                act.wait_ge(s["n_xT"], 1)
                nc.scalar.activation(hT[:, :], PB[0][:, :], ACT.Copy).then_inc(s["n_hT"], 1)
                if shared:
                    for c in range(2):
                        act.wait_ge(s["n_sgp"], c + 1)
                        nc.scalar.activation(sg[:, c, :], PB[2 + c][:, :], ACT.Silu).then_inc(s["n_sg"], 1)

            @block.tensor
            def _(pe):
                pe.wait_ge(s["n_h"], 1)
                for t in range(LT):
                    last = nc.tensor.transpose(PB[0][:, t * P:(t + 1) * P], xh[:, t, :], ident[:, :])
                last.then_inc(s["n_xT"], 1)
                pe.wait_ge(s["n_hT"], 1)
                for t in range(LT):
                    last = nc.tensor.matmul(PB[1][:, t * E:(t + 1) * E], hT[:, t * P:(t + 1) * P], wr[:, :],
                                            start=True, stop=True)
                last.then_inc(s["n_lg"], 1)
                if shared:
                    wg, wu, wd = shared
                    for c in range(2):
                        nc.tensor.matmul(PB[2 + c][:, :], wg[:, c * P:(c + 1) * P], hT[:, :],
                                         start=True, stop=True).then_inc(s["n_sgp"], 1)
                        nc.tensor.matmul(PB[4 + c][:, :], wu[:, c * P:(c + 1) * P], hT[:, :],
                                         start=True, stop=True).then_inc(s["n_sup"], 1)
                    pe.wait_ge(s["n_su"], 2)
                    for t in range(LT):
                        for c in range(2):
                            last = nc.tensor.matmul(PB[6][:, t * D:(t + 1) * D], su[:, c, t * P:(t + 1) * P],
                                                    wd[:, c, :], start=(c == 0), stop=(c == 1))
                    last.then_inc(s["n_so"], 1)

            if shared:
                @block.sync
                def _(sp):
                    sp.wait_ge(s["n_soe"], 1)
                    sp.dma_start(g["acc"][bass.ds(b * L, L), :].rearrange("(t p) d -> p t d", p=P), so[:, :, :])\
                      .then_inc(s["n_acc"], 16)
                    sp.wait_ge(s["n_h"], 1)
                    sp.dma_start(g["rows"][bass.ds(b * L, L), 0:D].rearrange("(t p) d -> p t d", p=P), xh[:, :, :])\
                      .then_inc(s["n_row"], 16)
                    sp.wait_ge(s["n_acc"], 16)
                    sp.wait_ge(s["n_row"], 16)
        s.end()


NORM_SEMS = ["n_ln", "n_var", "n_rstd", "n_h", "n_xT", "n_hT", "n_lg", "n_lge", "n_sgp", "n_sup", "n_sg",
             "n_su", "n_so", "n_soe", "n_acc", "n_row"]


def experts0(nc, g, a):
    PB, X, ident = g["PB"], g["X"], g["ident"]
    TE = NT * E0
    with ExitStack() as keep:
        sb = lambda n, sh, d=F32: keep.enter_context(nc.sbuf_tensor(n, sh, d))
        H = g["H"] = sb("H0", [P, NT, D])
        LG = g["LG"] = sb("LG0", [P, NT, E1])
        factor = sb("factor", [P, NT])
        slot = sb("slot", [P, NT], I32)
        with Stage(nc, ["c_w"]) as s:
            wr = keep.enter_context(nc.sbuf_tensor("wr", [D, E0], F32))
            with nc.Block() as block:
                @block.sync
                def _(sp):
                    sp.dma_start(wr[:, :], a["L0_ffn_Wr"]).then_inc(s["c_w"], 16)
                    sp.wait_ge(s["c_w"], 16)
            s.end()
        with Stage(nc, NORM_SEMS) as s:
            norm_router(nc, g, s, wr, E0)
        with Stage(nc, ["d_io", "d_sub", "d_exp", "d_oh", "d_cum", "d_dve", "d_slot", "d_sc", "d_pool"]) as s:
            rank = s.sb("rank", [P, E0])
            eid = s.sb("eid", [P, E0])
            mx = s.sb("mx", [P, NT])
            ex = s.sb("ex", [P, NT, E0])
            sm = s.sb("sm", [P, NT])
            key = s.sb("key", [P, NT, E0])
            oh = s.sb("oh", [P, NT, E0])
            ohb = s.sb("ohb", [P, NT, E0], BF16)
            tot = s.sb("tot", [P, E0, NT])
            msk = s.sb("msk", [P, E0, NT])
            inc = s.sb("inc", [P, E0, NT])
            pos = s.sb("pos", [P, NT, E0])
            own = s.sb("own", [P, NT])
            own2 = s.sb("own2", [P, NT])
            kept = s.sb("kept", [P, NT])
            with nc.Block() as block:
                @block.gpsimd
                def _(pool):
                    nc.gpsimd.iota(rank[:, :], pattern=[[-1, E0]], base=E0, channel_multiplier=0,
                                   allow_small_or_imprecise_dtypes=True).then_inc(s["d_io"], 1)
                    nc.gpsimd.iota(eid[:, :], pattern=[[CAP0, E0]], base=-1, channel_multiplier=0,
                                   allow_small_or_imprecise_dtypes=True).then_inc(s["d_io"], 1)
                    nc.gpsimd.memset(msk[:, :, :], 1.0).then_inc(s["d_pool"], 1)
                    pool.wait_ge(s["d_pool"], 1)
                    nc.gpsimd.memset(msk[:, :, 0:1], 0.0).then_inc(s["d_io"], 1)
                    pool.wait_ge(s["d_slot"], 1)
                    for t in range(NT):
                        nc.gpsimd.indirect_dma_start(
                            out=g["disp"], out_offset=bass.IndirectOffsetOnAxis(ap=slot[:, t:t + 1], axis=0),
                            in_=H[:, t, :], in_offset=None, bounds_check=SLOTS0 - 1, oob_is_err=False)\
                            .then_inc(s["d_sc"], 16)
                    pool.wait_ge(s["d_sc"], 16 * NT)

                @block.scalar
                def _(act):
                    act.wait_ge(s["d_sub"], 1)
                    nc.scalar.activation(ex[:, :, :], ex[:, :, :], ACT.Exp).then_inc(s["d_exp"], 1)

                @block.tensor
                def _(pe):
                    pe.wait_ge(s["d_oh"], 1)
                    rows = ohb[:, :, :].rearrange("p t e -> p (t e)")
                    nc.tensor.matmul(PB[0][:, 0:TE], g["tri"][:, :], rows, start=True, stop=True)
                    nc.tensor.matmul(PB[1][:, 0:TE], g["ones"][:, :], rows, start=True, stop=True)\
                        .then_inc(s["d_cum"], 1)

                @block.vector
                def _(dve):
                    link = linker(dve, s["d_dve"])
                    V = nc.vector
                    dve.wait_ge(s["d_io"], 3)
                    link(V.tensor_reduce(mx[:, :], LG[:, :, 0:E0], AX.X, ALU.max))
                    V.tensor_tensor(ex[:, :, :], LG[:, :, 0:E0], bcast(mx[:, :], 2, E0), ALU.subtract)\
                        .then_inc(s["d_sub"], 1)
                    link(V.tensor_tensor(key[:, :, :], LG[:, :, 0:E0], bcast(mx[:, :], 2, E0), ALU.is_equal))
                    link(V.tensor_tensor(key[:, :, :], key[:, :, :], bcast(rank[:, :], 1, NT), ALU.mult))
                    link(V.tensor_reduce(own[:, :], key[:, :, :], AX.X, ALU.max))
                    link(V.tensor_tensor(oh[:, :, :], key[:, :, :], bcast(own[:, :], 2, E0), ALU.is_equal))
                    V.tensor_copy(ohb[:, :, :], oh[:, :, :]).then_inc(s["d_oh"], 1)
                    dve.wait_ge(s["d_exp"], 1)
                    link(V.tensor_reduce(sm[:, :], ex[:, :, :], AX.X, ALU.add))
                    link(V.reciprocal(sm[:, :], sm[:, :]))
                    dve.wait_ge(s["d_cum"], 1)
                    te = lambda x: x.rearrange("p (t e) -> p t e", e=E0)
                    link(V.tensor_copy(tot[:, :, :].rearrange("p e t -> p t e"), te(PB[1][:, 0:TE])))
                    f = lambda x: x[:, :, :].rearrange("p e t -> p (e t)")
                    link(V.tensor_tensor_scan(f(inc), f(msk), f(tot), 0.0, ALU.mult, ALU.add))
                    link(V.tensor_tensor(inc[:, :, :], inc[:, :, :], tot[:, :, :], ALU.subtract))
                    link(V.tensor_tensor(pos[:, :, :], te(PB[0][:, 0:TE]),
                                         inc[:, :, :].rearrange("p e t -> p t e"), ALU.add))
                    link(V.tensor_tensor(key[:, :, :], pos[:, :, :], oh[:, :, :], ALU.mult))
                    link(V.tensor_reduce(own[:, :], key[:, :, :], AX.X, ALU.add))
                    link(V.tensor_tensor(key[:, :, :], oh[:, :, :], bcast(eid[:, :], 1, NT), ALU.mult))
                    link(V.tensor_reduce(own2[:, :], key[:, :, :], AX.X, ALU.add))
                    link(V.tensor_scalar(kept[:, :], own[:, :], float(CAP0), None, ALU.is_le))
                    link(V.scalar_tensor_tensor(factor[:, :], sm[:, :], -1.0, kept[:, :], ALU.add, ALU.mult))
                    link(V.tensor_scalar(factor[:, :], factor[:, :], 1.0, None, ALU.add))
                    link(V.tensor_tensor(own[:, :], own[:, :], own2[:, :], ALU.add))
                    link(V.tensor_scalar(kept[:, :], kept[:, :], -float(2 * SLOTS0), float(2 * SLOTS0),
                                         ALU.mult, ALU.add))
                    link(V.tensor_tensor(own[:, :], own[:, :], kept[:, :], ALU.add))
                    V.tensor_copy(slot[:, :], own[:, :]).then_inc(s["d_slot"], 1)
            s.end(pool_dmas=True)
        CT = CAP0 // P
        HF = CAP0 // 2
        with Stage(nc, ["e_w1", "e_w2", "e_in", "e_t", "e_te", "e_h", "e_ha", "e_hd", "e_o", "e_oe", "e_out"]) as s:
            w1 = [s.sb(f"w1_{i}", [D, F0]) for i in range(2)]
            w2 = [s.sb(f"w2_{i}", [P, F0 // P, D]) for i in range(2)]
            xin = [s.sb(f"xin{i}", [P, CT, D]) for i in range(2)]
            xT = s.sb("xT", [D, CAP0])
            hid = s.sb("hid", [P, F0 // P, CAP0])
            eo = s.sb("eo", [P, CT, D])

            def load(sp, i, e):
                sp.dma_start(w1[i][:, :], a["L0_ffn_W1"][bass.ds(e, 1), :, :].rearrange("o d f -> d (o f)"))\
                  .then_inc(s["e_w1"], 16)
                sp.dma_start(w2[i][:, :, :], a["L0_ffn_W2"][bass.ds(e, 1), :, :]
                             .rearrange("o (c p) d -> p (o c) d", p=P)).then_inc(s["e_w2"], 16)
                sp.dma_start(xin[i][:, :, :], g["disp"][bass.ds(e * CAP0, CAP0), :]
                             .rearrange("(t p) d -> p t d", p=P)).then_inc(s["e_in"], 16)

            def loaded(eng, n):
                eng.wait_ge(s["e_w1"], 16 * n)
                eng.wait_ge(s["e_w2"], 16 * n)
                eng.wait_ge(s["e_in"], 16 * n)
            with nc.Block() as block:
                @block.sync
                def _(sp):
                    load(sp, 0, 0)
                    loaded(sp, 1)
            s.end()
            with nc.Fori(0, E0 // 2) as pair:
                with nc.Block(no_gpsimd_drain=True) as block:
                    @block.sync
                    def _(sp):
                        load(sp, 1, pair * 2 + 1)
                        loaded(sp, 1)
                        for i in range(2):
                            sp.wait_ge(s["e_oe"], i + 1)
                            sp.dma_start(g["eout"][bass.ds((pair * 2 + i) * CAP0, CAP0), :]
                                         .rearrange("(t p) d -> p t d", p=P), eo[:, :, :]).then_inc(s["e_out"], 16)
                            if i == 0:
                                load(sp, 0, (pair + 1) % (E0 // 2) * 2)
                                loaded(sp, 2)
                        sp.wait_ge(s["e_out"], 32)

                    @block.tensor
                    def _(pe):
                        for i in range(2):
                            if i == 1:
                                loaded(pe, 1)
                                pe.wait_ge(s["e_oe"], 1)
                            for t in range(CT):
                                last = nc.tensor.transpose(PB[t // 4][:, t % 4 * P:(t % 4 + 1) * P],
                                                           xin[i][:, t, :], ident[:, :])
                            last.then_inc(s["e_t"], 1)
                            pe.wait_ge(s["e_te"], i + 1)
                            for n in range(2 * F0 // P):
                                c, u = n // 2, n % 2
                                m = i * 2 * F0 // P + n
                                if m >= 4:
                                    pe.wait_ge(s["e_ha"] if m % 2 == 0 else s["e_hd"], (m - 4) // 2 + 1)
                                nc.tensor.matmul(PB[2 + n % 4][:, 0:HF], w1[i][:, c * P:(c + 1) * P],
                                                 xT[:, u * HF:(u + 1) * HF], start=True, stop=True)\
                                    .then_inc(s["e_h"], 1)
                            pe.wait_ge(s["e_ha"], (i + 1) * F0 // P)
                            pe.wait_ge(s["e_hd"], (i + 1) * F0 // P)
                            for t in range(CT):
                                for c in range(F0 // P):
                                    last = nc.tensor.matmul(PB[6 + t // 4][:, t % 4 * D:(t % 4 + 1) * D],
                                                            hid[:, c, t * P:(t + 1) * P], w2[i][:, c, :],
                                                            start=(c == 0), stop=(c == F0 // P - 1))
                            last.then_inc(s["e_o"], 1)

                    @block.scalar
                    def _(act):
                        for i in range(2):
                            for n in range(0, 2 * F0 // P, 2):
                                act.wait_ge(s["e_h"], i * 2 * F0 // P + n + 1)
                                nc.scalar.activation(hid[:, n // 2, 0:HF], PB[2 + n % 4][:, 0:HF], ACT.Relu)\
                                    .then_inc(s["e_ha"], 1)

                    @block.vector
                    def _(dve):
                        for i in range(2):
                            dve.wait_ge(s["e_t"], i + 1)
                            nc.vector.tensor_copy(xT[:, 0:4 * P], PB[0][:, :])
                            nc.vector.tensor_copy(xT[:, 4 * P:CAP0], PB[1][:, 0:CAP0 - 4 * P])\
                                .then_inc(s["e_te"], 1)
                            for n in range(1, 2 * F0 // P, 2):
                                dve.wait_ge(s["e_h"], i * 2 * F0 // P + n + 1)
                                nc.vector.tensor_scalar(hid[:, n // 2, HF:CAP0], PB[2 + n % 4][:, 0:HF], 0.0,
                                                        None, ALU.max).then_inc(s["e_hd"], 1)
                            dve.wait_ge(s["e_o"], i + 1)
                            if i == 1:
                                dve.wait_ge(s["e_out"], 16)
                            nc.vector.tensor_copy(eo[:, 0:4, :], PB[6][:, :].rearrange("p (t d) -> p t d", t=4))
                            nc.vector.tensor_copy(eo[:, 4:CT, :], PB[7][:, 0:CAP0 - 4 * P]
                                                  .rearrange("p (t d) -> p t d", d=D)).then_inc(s["e_oe"], 1)
                s.end()
        with Stage(nc, ["f_g", "f_m", "f_x"]) as s:
            with nc.Block() as block:
                @block.gpsimd
                def _(pool):
                    for t in range(NT):
                        nc.gpsimd.indirect_dma_start(
                            out=H[:, t, :], out_offset=None, in_=g["eout"],
                            in_offset=bass.IndirectOffsetOnAxis(ap=slot[:, t:t + 1], axis=0),
                            bounds_check=SLOTS0 - 1, oob_is_err=False).then_inc(s["f_g"], 16)
                    pool.wait_ge(s["f_g"], 16 * NT)
            s.end(pool_dmas=True)
            with nc.Block() as block:
                @block.vector
                def _(dve):
                    link = linker(dve, s["f_x"])
                    for b in range(B):
                        for t in range(b * LT, (b + 1) * LT):
                            link(nc.vector.scalar_tensor_tensor(H[:, t, :], H[:, t, :], factor[:, t:t + 1],
                                                                g["MODB"][:, b, GB, :], ALU.mult, ALU.mult))
                    link(nc.vector.tensor_tensor(X[:, :, :], X[:, :, :], H[:, :, :], ALU.add))
            s.end()


ROW1 = D + E1


def count_along(nc, dve, link, f, mask, msk, tot, inc, out, te, hold):
    V = nc.vector
    link(V.tensor_copy(tot[:, :, :].rearrange("p e t -> p t e"), te(hold[1])))
    link(V.tensor_tensor_scan(f(inc), f(msk), f(tot), 0.0, ALU.mult, ALU.add))
    link(V.tensor_tensor(inc[:, :, :], inc[:, :, :], tot[:, :, :], ALU.subtract))
    link(V.tensor_tensor(out[:, :, :], te(hold[0]), inc[:, :, :].rearrange("p e t -> p t e"), ALU.add))


def experts1(nc, g, a):
    PB, X, ident = g["PB"], g["X"], g["ident"]
    FC = F1 // P
    JC = CAP1 // P
    NA_, NB_ = 16, 32
    with ExitStack() as keep:
        sb = lambda n, sh, d=F32: keep.enter_context(nc.sbuf_tensor(n, sh, d))
        H = g["H"] = sb("H1", [P, NT, D])
        LG = g["LG"] = sb("LG1", [P, NT, E1])
        wr = sb("wr1", [D, E1])
        wg = sb("wg", [D, SH])
        wu = sb("wu", [D, SH])
        wd = sb("wd", [P, SH // P, D])
        biasT = sb("biasT", [P, 2, E1, FC])
        dbias = sb("dbias", [P, E1, D])
        ids = sb("ids", [P, E1, JC], I32)
        with Stage(nc, ["g_ld", "g_t", "g_e"]) as s:
            gl = s.sb("gl", [E1, D])
            l1 = s.sb("l1", [P, 2, D])
            l2 = s.sb("l2", [P, 2, D])
            l3 = s.sb("l3", [D, SH])
            lb = s.sb("lb", [E1 * FC, 2, P])
            with nc.Block() as block:
                @block.sync
                def _(sp):
                    for d, v in ((gl[:, :], a["L1_ffn_gate_w"]),
                                 (l1[:, :, :], a["L1_ffn_sh_gate_w"].rearrange("(c p) d -> p c d", p=P)),
                                 (l2[:, :, :], a["L1_ffn_sh_up_w"].rearrange("(c p) d -> p c d", p=P)),
                                 (l3[:, :], a["L1_ffn_sh_down_w"]),
                                 (lb[:, 0, :], a["L1_ffn_up_b"].rearrange("e (c p) -> (e c) p", p=P)),
                                 (lb[:, 1, :], a["L1_ffn_gb"].rearrange("e (c p) -> (e c) p", p=P)),
                                 (dbias[:, :, :], bcast(a["L1_ffn_down_b"], 0, P))):
                        sp.dma_start(d, v).then_inc(s["g_ld"], 16)
                    sp.wait_ge(s["g_ld"], 7 * 16)

                @block.tensor
                def _(pe):
                    pe.wait_ge(s["g_ld"], 7 * 16)
                    T = nc.tensor.transpose
                    T(PB[0][:, 0:E1], gl[:, :], ident[0:E1, 0:E1])
                    for c in range(2):
                        T(PB[1][:, c * P:(c + 1) * P], l1[:, c, :], ident[:, :])
                        T(PB[2][:, c * P:(c + 1) * P], l2[:, c, :], ident[:, :])
                        T(PB[3][:, c * P:(c + 1) * P], l3[:, c * P:(c + 1) * P], ident[:, :])
                        last = T(PB[4][:, c * E1 * FC:(c + 1) * E1 * FC], lb[:, c, :],
                                 ident[0:E1 * FC, 0:E1 * FC])
                    last.then_inc(s["g_t"], 1)

                @block.vector
                def _(dve):
                    dve.wait_ge(s["g_t"], 1)
                    V = nc.vector
                    V.tensor_copy(wr[:, :], PB[0][:, 0:E1])
                    V.tensor_copy(wg[:, :], PB[1][:, 0:SH])
                    V.tensor_copy(wu[:, :], PB[2][:, 0:SH])
                    V.tensor_copy(wd[:, :, :], PB[3][:, 0:SH].rearrange("p (c d) -> p c d", c=2))
                    V.tensor_copy(biasT[:, :, :, :], PB[4][:, 0:2 * E1 * FC]
                                  .rearrange("p (k e c) -> p k e c", k=2, c=FC)).then_inc(s["g_e"], 1)
                    dve.wait_ge(s["g_e"], 1)
            s.end()
        with Stage(nc, NORM_SEMS) as s:
            norm_router(nc, g, s, wr, E1, shared=(wg, wu, wd))
        TE = NT * E1
        BITS = 30
        with Stage(nc, ["h_sig", "h_io", "h_pool", "h_dve", "h_m", "h_cnt", "h_c", "h_cum", "h_ab", "h_id",
                        "h_ide", "h_st", "h_ids", "h_row"]) as s:
            T = s.sb("T", [P, E1], I32)
            cand = s.sb("cand", [P, E1], I32)
            take = s.sb("take", [P, E1], I32)
            cnt = s.sb("cnt", [P, E1])
            m = s.sb("m", [P, NT, E1], BF16)
            gt = s.sb("gt", [P, NT, E1])
            eq = s.sb("eq", [P, NT, E1])
            tot = s.sb("tot1", [P, E1, NT])
            msk = s.sb("msk1", [P, E1, NT])
            inc = s.sb("inc1", [P, E1, NT])
            cum = s.sb("cum1", [P, NT, E1])
            posi = s.sb("posi", [P, NT, E1], I32)
            ai = s.sb("ai", [P, NT, E1], I32)
            af = s.sb("af", [P, NT, E1])
            bf = s.sb("bf", [P, NT, E1])
            ioa = s.sb("ioa", [P, NA_])
            iob = s.sb("iob", [P, NB_])
            iot = s.sb("iot", [P, NT])
            pid = s.sb("pid", [P, 1])
            A = s.sb("A", [P, NT, E1, NA_], BF16)
            A2 = s.sb("A2", [P, NT, E1, NA_], BF16)
            Bo = s.sb("Bo", [P, NT, E1, NB_], BF16)
            Bp = s.sb("Bp", [P, NT, E1, NB_], BF16)
            idf = s.sb("idf", [NA_, E1, NB_], I32)
            f = lambda x: x[:, :, :].rearrange("p e t -> p (e t)")
            te = lambda x: x[:, :].rearrange("p (t e) -> p t e", e=E1)
            flat = m[:, :, :].rearrange("p t e -> p (t e)")
            with nc.Block() as block:
                @block.scalar
                def _(act):
                    nc.scalar.activation(LG[:, :, :], LG[:, :, :], ACT.Sigmoid).then_inc(s["h_sig"], 1)

                @block.sync
                def _(sp):
                    sp.wait_ge(s["h_sig"], 1)
                    sp.dma_start(g["rows"][:, D:ROW1].rearrange("(t p) e -> p t e", p=P), LG[:, :, :])\
                      .then_inc(s["h_row"], 16)
                    sp.wait_ge(s["h_ide"], 1)
                    sp.dma_start(g["ids"].rearrange("(e a b) -> a e b", e=E1, a=NA_), idf[:, :, :])\
                      .then_inc(s["h_st"], 16)
                    sp.wait_ge(s["h_st"], 16)
                    sp.dma_start(ids[:, :, :], g["ids"].rearrange("(e p j) -> p e j", e=E1, p=P))\
                      .then_inc(s["h_ids"], 16)
                    sp.wait_ge(s["h_ids"], 16)
                    sp.wait_ge(s["h_row"], 16)

                @block.gpsimd
                def _(pool):
                    io = dict(allow_small_or_imprecise_dtypes=True)
                    G = nc.gpsimd
                    G.iota(ioa[:, :], pattern=[[1, NA_]], base=0, channel_multiplier=0, **io).then_inc(s["h_io"], 1)
                    G.iota(iob[:, :], pattern=[[1, NB_]], base=0, channel_multiplier=0, **io).then_inc(s["h_io"], 1)
                    G.iota(iot[:, :], pattern=[[P, NT]], base=0, channel_multiplier=0, **io).then_inc(s["h_io"], 1)
                    G.iota(pid[:, :], pattern=[[0, 1]], base=0, channel_multiplier=1, **io).then_inc(s["h_io"], 1)
                    G.memset(T[:, :], 0).then_inc(s["h_io"], 1)
                    G.memset(msk[:, :, :], 1.0).then_inc(s["h_pool"], 1)
                    pool.wait_ge(s["h_pool"], 1)
                    G.memset(msk[:, :, 0:1], 0.0).then_inc(s["h_io"], 1)

                @block.vector
                def _(dve):
                    link = linker(dve, s["h_dve"])
                    V = nc.vector
                    dve.wait_ge(s["h_sig"], 1)
                    dve.wait_ge(s["h_io"], 6)
                    for n in range(BITS):
                        link(V.tensor_scalar(cand[:, :], T[:, :], 1 << (BITS - 1 - n), None, ALU.bitwise_or))
                        V.tensor_tensor(m[:, :, :], LG[:, :, :], bcast(cand[:, :].bitcast(F32), 1, NT), ALU.is_ge)\
                            .then_inc(s["h_m"], 1)
                        dve.wait_ge(s["h_cnt"], n + 1)
                        link(V.tensor_reduce(cnt[:, :], PB[n % 2][:, :].rearrange("p (t e) -> p e t", e=E1),
                                             AX.X, ALU.add))
                        link(V.tensor_scalar(take[:, :], cnt[:, :], float(CAP1), None, ALU.is_ge))
                        link(V.copy_predicated(T[:, :], take[:, :], cand[:, :]))
                    Tf = bcast(T[:, :].bitcast(F32), 1, NT)
                    link(V.tensor_tensor(gt[:, :, :], LG[:, :, :], Tf, ALU.is_gt))
                    V.tensor_copy(m[:, :, :], gt[:, :, :]).then_inc(s["h_m"], 1)
                    dve.wait_ge(s["h_cnt"], BITS + 1)
                    link(V.tensor_reduce(cnt[:, :], PB[2][:, :].rearrange("p (t e) -> p e t", e=E1), AX.X, ALU.add))
                    link(V.tensor_scalar(cnt[:, :], cnt[:, :], -1.0, float(CAP1), ALU.mult, ALU.add))
                    link(V.tensor_tensor(eq[:, :, :], LG[:, :, :], Tf, ALU.is_equal))
                    V.tensor_copy(m[:, :, :], eq[:, :, :]).then_inc(s["h_m"], 1)
                    dve.wait_ge(s["h_cum"], 1)
                    count_along(nc, dve, link, f, m, msk, tot, inc, cum, te, PB[3:5])
                    link(V.tensor_tensor(cum[:, :, :], cum[:, :, :], bcast(cnt[:, :], 1, NT), ALU.is_le))
                    link(V.tensor_tensor(eq[:, :, :], eq[:, :, :], cum[:, :, :], ALU.mult))
                    link(V.tensor_tensor(gt[:, :, :], gt[:, :, :], eq[:, :, :], ALU.add))
                    V.tensor_copy(m[:, :, :], gt[:, :, :]).then_inc(s["h_m"], 1)
                    dve.wait_ge(s["h_cum"], 2)
                    count_along(nc, dve, link, f, m, msk, tot, inc, cum, te, PB[5:7])
                    link(V.tensor_tensor(cum[:, :, :], cum[:, :, :], gt[:, :, :], ALU.mult))
                    link(V.tensor_tensor(cum[:, :, :], cum[:, :, :], gt[:, :, :], ALU.subtract))
                    link(V.tensor_copy(posi[:, :, :], cum[:, :, :]))
                    link(V.tensor_scalar(ai[:, :, :], posi[:, :, :], 5, None, ALU.logical_shift_right))
                    link(V.tensor_scalar(posi[:, :, :], posi[:, :, :], NB_ - 1, None, ALU.bitwise_and))
                    link(V.tensor_copy(af[:, :, :], ai[:, :, :]))
                    link(V.tensor_copy(bf[:, :, :], posi[:, :, :]))
                    link(V.scalar_tensor_tensor(af[:, :, :], af[:, :, :], 1.0, gt[:, :, :], ALU.add, ALU.mult))
                    link(V.tensor_scalar(af[:, :, :], af[:, :, :], -1.0, None, ALU.add))
                    q = lambda x: x[:, :, :].rearrange("p t e -> p (t e)")
                    q4 = lambda x: x[:, :, :, :].rearrange("p t e n -> p (t e) n")
                    link(V.tensor_tensor(q4(A), bcast(q(af), 2, NA_), bcast(ioa[:, :], 1, TE), ALU.is_equal))
                    V.tensor_tensor(q4(Bo), bcast(q(bf), 2, NB_), bcast(iob[:, :], 1, TE), ALU.is_equal)\
                        .then_inc(s["h_ab"], 1)
                    dve.wait_ge(s["h_ab"], 1)
                    V.tensor_scalar(q4(Bp), q4(Bo), pid[:, 0:1], None, ALU.mult)
                    V.tensor_tensor(A2[:, :, :, :].rearrange("p t e n -> p t (e n)"),
                                    A[:, :, :, :].rearrange("p t e n -> p t (e n)"),
                                    bcast(iot[:, :], 2, E1 * NA_), ALU.mult).then_inc(s["h_ab"], 1)
                    dve.wait_ge(s["h_id"], 1)
                    V.tensor_copy(idf[:, :, :], PB[7][0:NA_, :].rearrange("a (e b) -> a e b", b=NB_))\
                        .then_inc(s["h_ide"], 1)

                @block.tensor
                def _(pe):
                    def count(lhs, bank):
                        return nc.tensor.matmul(bank[:, :], lhs[:, :], flat, start=True, stop=True)
                    for n in range(BITS):
                        pe.wait_ge(s["h_m"], n + 1)
                        count(g["ones"], PB[n % 2]).then_inc(s["h_cnt"], 1)
                    pe.wait_ge(s["h_m"], BITS + 1)
                    count(g["ones"], PB[2]).then_inc(s["h_cnt"], 1)
                    for n in range(2):
                        pe.wait_ge(s["h_m"], BITS + 2 + n)
                        count(g["tri"], PB[3 + 2 * n])
                        count(g["ones"], PB[4 + 2 * n]).then_inc(s["h_cum"], 1)
                    pe.wait_ge(s["h_ab"], 2)
                    for e in range(E1):
                        o = PB[7][0:NA_, e * NB_:(e + 1) * NB_]
                        for t in range(NT):
                            nc.tensor.matmul(o, A[:, t, e, :], Bp[:, t, e, :], start=(t == 0), stop=False)
                            last = nc.tensor.matmul(o, A2[:, t, e, :], Bo[:, t, e, :], start=False,
                                                    stop=(t == NT - 1))
                    last.then_inc(s["h_id"], 1)
            s.end()
        with Stage(nc, ["i_up", "i_gw", "i_dw", "i_id", "i_rows", "i_bi", "i_t", "i_td", "i_ta", "i_u", "i_g",
                        "i_sg", "i_h", "i_o", "i_od", "i_oe", "i_add"]) as s:
            up = [s.sb(f"up{i}", [P, FC, D]) for i in range(2)]
            gw = [s.sb(f"gw{i}", [P, FC, D]) for i in range(2)]
            dw = [s.sb(f"dw{i}", [D, F1]) for i in range(2)]
            xg = [s.sb(f"xg{i}", [P, JC, ROW1]) for i in range(2)]
            idx = [s.sb(f"idx{i}", [P, JC], I32) for i in range(2)]
            scr = s.sb("scr", [P, 2, JC])
            bi = s.sb("bi", [P, 2, 2, FC])
            db = s.sb("db", [P, 2, D])
            xT = s.sb("xT1", [D, CAP1])
            upT = s.sb("upT", [D, F1])
            gwT = s.sb("gwT", [D, F1])
            dwT = s.sb("dwT", [P, FC, D])
            sg = s.sb("sg1", [P, FC, CAP1])
            hid = s.sb("hid1", [P, FC, CAP1])
            eo = s.sb("eo1", [P, JC, D])

            def weights(sp, i, e):
                w3 = lambda n: a[n][bass.ds(e, 1), :, :].rearrange("o (c p) d -> p (o c) d", p=P)
                sp.dma_start(up[i][:, :, :], w3("L1_ffn_up_w")).then_inc(s["i_up"], 16)
                sp.dma_start(gw[i][:, :, :], w3("L1_ffn_gw")).then_inc(s["i_gw"], 16)
                sp.dma_start(dw[i][:, :], a["L1_ffn_down_w"][bass.ds(e, 1), :, :]
                             .rearrange("o d f -> d (o f)")).then_inc(s["i_dw"], 16)

            def rows(pool, i, e, n):
                nc.gpsimd.tensor_copy(idx[i][:, :], ids[:, bass.ds(e, 1), :].rearrange("p o j -> p (o j)"))\
                    .then_inc(s["i_id"], 1)
                pool.wait_ge(s["i_id"], n)
                for j in range(JC):
                    nc.gpsimd.indirect_dma_start(
                        out=xg[i][:, j, :], out_offset=None, in_=g["rows"],
                        in_offset=bass.IndirectOffsetOnAxis(ap=idx[i][:, j:j + 1], axis=0),
                        bounds_check=B * L - 1, oob_is_err=False).then_inc(s["i_rows"], 16)

            def loaded(eng, n):
                eng.wait_ge(s["i_up"], 16 * n)
                eng.wait_ge(s["i_gw"], 16 * n)
                eng.wait_ge(s["i_dw"], 16 * n)

            with nc.Block() as block:
                @block.sync
                def _(sp):
                    weights(sp, 0, 0)
                    loaded(sp, 1)

                @block.gpsimd
                def _(pool):
                    rows(pool, 0, 0, 1)
                    pool.wait_ge(s["i_rows"], 16 * JC)
            s.end(pool_dmas=True)
            with nc.Fori(0, E1 // 2) as pair:
                with nc.Block(no_gpsimd_drain=True) as block:
                    @block.sync
                    def _(sp):
                        weights(sp, 1, pair * 2 + 1)
                        loaded(sp, 1)
                        sp.wait_ge(s["i_t"], 1)
                        weights(sp, 0, (pair + 1) % (E1 // 2) * 2)
                        loaded(sp, 2)

                    @block.gpsimd
                    def _(pool):
                        def add(i):
                            pool.wait_ge(s["i_oe"], i + 1)
                            for j in range(JC):
                                nc.gpsimd.indirect_dma_start(
                                    out=g["acc"], out_offset=bass.IndirectOffsetOnAxis(ap=scr_idx[i][:, j:j + 1],
                                                                                       axis=0),
                                    in_=eo[:, j, :], in_offset=None, bounds_check=B * L - 1, oob_is_err=True,
                                    compute_op=ALU.add).then_inc(s["i_add"], 16)
                            pool.wait_ge(s["i_add"], 16 * JC * (i + 1))
                        rows(pool, 1, pair * 2 + 1, 1)
                        scr_idx = idx
                        add(0)
                        pool.wait_ge(s["i_rows"], 16 * JC)
                        rows(pool, 0, (pair + 1) % (E1 // 2) * 2, 2)
                        add(1)
                        pool.wait_ge(s["i_rows"], 16 * 2 * JC)

                    @block.tensor
                    def _(pe):
                        TR = nc.tensor.transpose
                        for i in range(2):
                            if i == 1:
                                loaded(pe, 1)
                                pe.wait_ge(s["i_rows"], 16 * JC)
                                pe.wait_ge(s["i_oe"], 1)
                            for c in range(FC):
                                TR(PB[1][:, c * P:(c + 1) * P], up[i][:, c, :], ident[:, :])
                                TR(PB[2][:, c * P:(c + 1) * P], gw[i][:, c, :], ident[:, :])
                                TR(PB[3][:, c * P:(c + 1) * P], dw[i][:, c * P:(c + 1) * P], ident[:, :])
                                last = TR(PB[0][:, c * P:(c + 1) * P], xg[i][:, c, 0:D], ident[:, :])
                            last.then_inc(s["i_t"], 1)
                            pe.wait_ge(s["i_td"], i + 1)
                            pe.wait_ge(s["i_ta"], i + 1)
                            for c in range(FC):
                                m = i * FC + c
                                if m >= 2:
                                    pe.wait_ge(s["i_h"], m - 1)
                                nc.tensor.matmul(PB[6 + c % 2][:, :], gwT[:, c * P:(c + 1) * P], xT[:, :],
                                                 start=True, stop=True).then_inc(s["i_g"], 1)
                                nc.tensor.matmul(PB[4 + c % 2][:, :], upT[:, c * P:(c + 1) * P], xT[:, :],
                                                 start=True, stop=True).then_inc(s["i_u"], 1)
                            pe.wait_ge(s["i_h"], (i + 1) * FC)
                            for j in range(JC):
                                for c in range(FC):
                                    last = nc.tensor.matmul(PB[0][:, j * D:(j + 1) * D],
                                                            hid[:, c, j * P:(j + 1) * P], dwT[:, c, :],
                                                            start=(c == 0), stop=(c == FC - 1))
                            last.then_inc(s["i_o"], 1)

                    @block.scalar
                    def _(act):
                        for i in range(2):
                            act.wait_ge(s["i_t"], i + 1)
                            nc.scalar.activation(gwT[:, :], PB[2][:, :], ACT.Copy)
                            nc.scalar.activation(dwT[:, :, :], PB[3][:, :].rearrange("p (c d) -> p c d", c=FC),
                                                 ACT.Copy).then_inc(s["i_ta"], 1)
                            act.wait_ge(s["i_bi"], 2)
                            for c in range(FC):
                                act.wait_ge(s["i_g"], i * FC + c + 1)
                                if i == 1:
                                    act.wait_ge(s["i_h"], c + 1)
                                nc.scalar.activation(sg[:, c, :], PB[6 + c % 2][:, :], ACT.Silu,
                                                     bias=bi[:, i, 1, c:c + 1]).then_inc(s["i_sg"], 1)

                    @block.vector
                    def _(dve):
                        V = nc.vector
                        for i in range(2):
                            V.tensor_copy(bi[:, i, :, :], biasT[:, :, bass.ds(pair * 2 + i, 1), :]
                                          .rearrange("p k o c -> p (k o) c")).then_inc(s["i_bi"], 1)
                            V.tensor_copy(db[:, i, :], dbias[:, bass.ds(pair * 2 + i, 1), :]
                                          .rearrange("p o d -> p (o d)"))
                        dve.wait_ge(s["i_bi"], 2)
                        for i in range(2):
                            dve.wait_ge(s["i_t"], i + 1)
                            V.tensor_copy(upT[:, :], PB[1][:, :])
                            V.tensor_copy(scr[:, i, :], xg[i][:, :, bass.ds(pair * 2 + (D + i), 1)]
                                          .rearrange("p j o -> p (j o)"))
                            V.tensor_copy(xT[:, :], PB[0][:, :]).then_inc(s["i_td"], 1)
                            for c in range(FC):
                                dve.wait_ge(s["i_u"], i * FC + c + 1)
                                dve.wait_ge(s["i_sg"], i * FC + c + 1)
                                V.scalar_tensor_tensor(hid[:, c, :], PB[4 + c % 2][:, :], bi[:, i, 0, c:c + 1],
                                                       sg[:, c, :], ALU.add, ALU.mult).then_inc(s["i_h"], 1)
                            dve.wait_ge(s["i_o"], i + 1)
                            if i == 1:
                                dve.wait_ge(s["i_add"], 16 * JC)
                            V.tensor_tensor(eo[:, :, :], PB[0][:, :].rearrange("p (j d) -> p j d", j=JC),
                                            bcast(db[:, i, :], 1, JC), ALU.add).then_inc(s["i_od"], 1)
                            dve.wait_ge(s["i_od"], i + 1)
                            V.tensor_tensor(eo[:, :, :], eo[:, :, :], bcast(scr[:, i, :], 2, D), ALU.mult)\
                                .then_inc(s["i_oe"], 1)
                s.end(pool_dmas=True)
        with Stage(nc, ["j_ld", "j_x"]) as s:
            with nc.Block() as block:
                @block.sync
                def _(sp):
                    sp.dma_start(H[:, :, :], g["acc"].rearrange("(t p) d -> p t d", p=P)).then_inc(s["j_ld"], 16)

                @block.vector
                def _(dve):
                    link = linker(dve, s["j_x"])
                    dve.wait_ge(s["j_ld"], 16)
                    hb = lambda x: x[:, :, :].rearrange("p (b t) d -> p b t d", b=B)
                    link(nc.vector.tensor_tensor(hb(H), hb(H), bcast(g["MODB"][:, :, GB, :], 2, LT), ALU.mult))
                    link(nc.vector.tensor_tensor(X[:, :, :], X[:, :, :], H[:, :, :], ALU.add))
            s.end()


def delta1(nc, g, a):
    PB, X, ident = g["PB"], g["X"], g["ident"]
    BA, BB = [PB[i] for i in (0, 1, 4, 5)], [PB[i] for i in (2, 3, 6, 7)]
    V, G, TE_ = nc.vector, nc.gpsimd, nc.tensor
    SQ = DK ** -0.5
    Q4 = HV // 4
    BS = 16
    PAD = KS - 1
    with ExitStack() as keep:
        sb = lambda n, sh, d=F32: keep.enter_context(nc.sbuf_tensor(n, sh, d))
        Wc = sb("Wc", [D, KS, CD])
        Wz = sb("Wz", [D, VD])
        Wab = sb("Wab", [D, 2 * HV])
        Wo = sb("Wo", [P, VD // P, D])
        dtb = sb("dtb", [P, HV])
        nA = sb("nA", [P, HV])
        nw = sb("nw", [P, DK])
        onesf = sb("onesf", [P, P])
        trif = sb("trif", [P, P])
        identz = sb("identz", [P, P])
        I4 = sb("I4", [P, 4, P])
        offm = sb("offm", [P, P])
        bm = sb("bm", [P, P // BS])
        d16 = sb("d16", [P, BS])
        bone = sb("bone", [P, P])
        hm = sb("hm", [P, 2])
        with Stage(nc, ["k_ld", "k_ex", "k_v", "k_g", "k_pe"]) as s:
            wq = s.sb("wqkv", [D, CD])
            cw = s.sb("cw", [P, CD, KS])
            with nc.Block() as block:
                @block.sync
                def _(sp):
                    for d, v in ((wq[:, :], a["L1_attn_W_qkv"]), (Wz[:, :], a["L1_attn_W_z"]),
                                 (Wab[:, 0:HV], a["L1_attn_W_b"]), (Wab[:, HV:2 * HV], a["L1_attn_W_a"]),
                                 (Wo[:, :, :], a["L1_attn_W_out"].rearrange("(c p) d -> p c d", p=P)),
                                 (dtb[:, :], bcast(a["L1_attn_dt_bias"], 0, P)),
                                 (nA[:, :], bcast(a["L1_attn_A_log"], 0, P)),
                                 (nw[:, :], bcast(a["L1_attn_norm_w"], 0, P)),
                                 (cw[:, :, :], bcast(a["L1_attn_conv_w"], 0, P))):
                        sp.dma_start(d, v).then_inc(s["k_ld"], 16)
                    sp.wait_ge(s["k_ld"], 9 * 16)

                @block.scalar
                def _(act):
                    act.wait_ge(s["k_ld"], 9 * 16)
                    nc.scalar.activation(nA[:, :], nA[:, :], ACT.Exp).then_inc(s["k_ex"], 1)

                @block.vector
                def _(dve):
                    link = linker(dve, s["k_v"])
                    dve.wait_ge(s["k_ld"], 9 * 16)
                    for i in range(KS):
                        V.tensor_tensor(Wc[:, i, :], wq[:, :], cw[:, :, i], ALU.mult)
                    dve.wait_ge(s["k_ex"], 1)
                    link(V.tensor_scalar(nA[:, :], nA[:, :], -1.0, None, ALU.mult))
                    dve.wait_ge(s["k_g"], 6)
                    for i in range(4):
                        V.tensor_copy(I4[:, i, :], ident[:, :])
                    V.tensor_copy(identz[:, 1:P], ident[:, 1:P])
                    link(V.tensor_scalar(offm[:, :], bone[:, :], -1.0, 1.0, ALU.mult, ALU.add))
                    link(V.tensor_reduce(d16[:, :], ident[:, :].rearrange("p (c i) -> p i c", i=BS), AX.X, ALU.add))
                    h4 = bm[:, :].rearrange("p (c i) -> p i c", i=2)
                    link(V.tensor_reduce(hm[:, :], h4, AX.X, ALU.add))

                @block.gpsimd
                def _(pool):
                    link = linker(pool, s["k_g"])
                    link(G.memset(onesf[:, :], 1.0))
                    link(G.memset(identz[:, :], 0.0))
                    link(G.affine_select(out=trif[:, :], in_=onesf[:, :], compare_op=ALU.is_ge, fill=0.0,
                                         base=0, pattern=[[1, P]], channel_multiplier=-1))
                    link(G.affine_select(out=bm[:, :], in_=onesf[:, 0:P // BS], compare_op=ALU.is_ge, fill=0.0,
                                         base=0, pattern=[[-BS, P // BS]], channel_multiplier=1))
                    link(G.affine_select(out=bm[:, :], in_=bm[:, :], compare_op=ALU.is_ge, fill=0.0,
                                         base=BS - 1, pattern=[[BS, P // BS]], channel_multiplier=-1))
                    link(G.tensor_copy(bone[:, :].rearrange("p (c i) -> p c i", i=BS), bcast(bm[:, :], 2, BS)))
            s.end()
        hT = sb("hTp", [D, PAD + L])
        S = sb("Sbd", [P, Q4, 4 * DK])
        gates = sb("gates", [P, LT, 4, HV])
        AL, BE, GM, GC = range(4)
        with Stage(nc, ["l_ln", "l_var", "l_rstd", "l_mc", "l_xn", "l_xT", "l_hT", "l_ab", "l_y", "l_ey", "l_g",
                        "l_cs", "l_al", "l_gc", "l_pz"]) as r, \
             Stage(nc, ["t_h", "t_ha", "t_qkv", "t_silu", "t_ss", "t_sq", "t_v", "t_qkn", "t_tq", "t_tqa", "t_tqd",
                        "t_kq", "t_al", "t_L", "t_Ls", "t_A", "t_P", "t_AT", "t_ATe", "t_acp", "t_R",
                        "t_DB", "t_DBe", "t_T16", "t_Tp", "t_Tpe", "t_N", "t_Ne", "t_Nt", "t_Nta", "t_Ntd",
                        "t_N2", "t_N2e", "t_N2t", "t_N2te", "t_R1", "t_R1e", "t_N4", "t_N4e", "t_R2", "t_R2e",
                        "t_T", "t_Te", "t_KS", "t_X", "t_W", "t_U", "t_U2", "t_QS", "t_PU", "t_O", "t_dS",
                        "t_z", "t_za", "t_on", "t_or", "t_of", "t_oT", "t_oTe", "t_out", "t_s", "t_pl"]) as s:
            st = r.sb("st", [P, LT, 6])
            mv = r.sb("mv", [P, LT, 2])
            rstd = r.sb("rstd", [P, LT])
            xh = r.sb("xh", [P, LT, D])
            mc = r.sb("mc", [P, 6])
            G64 = [P, LT, HV]
            sp_x, sp_y, sp_s, sp_p, sp_g, ab = [r.sb(n, G64) for n in ("spx", "spy", "sps", "spp", "spg", "ab")]
            hw = s.sb("hw", [D, PAD + P])
            gs = s.sb("gs", [P, 4, HV])
            qkv = s.sb("qkv", [P, CD])
            zs = s.sb("zs", [P, HV, DK])
            sq = s.sb("sq", [P, HV, DK])
            rn = s.sb("rn", [P, HV])
            KT = s.sb("KT", [P, Q4, P])
            QT = s.sb("QT", [P, Q4, P])
            KB = s.sb("KB", [P, Q4, 2, P])
            QB = s.sb("QB", [P, Q4, 2, P])
            big = [P, HV, P]
            Lt, At, Pt, Aoff, Tt16 = [s.sb(n, big) for n in ("Lt", "At", "Pt", "Aoff", "Tt16")]
            dl = s.sb("dl", [P, HV])
            NN = s.sb("NN", [P, 2, HV, P])
            IR = s.sb("IR", [P, 2, HV, P])
            N, Nt, IN, N2 = NN[:, 0, :, :], NN[:, 1, :, :], IR[:, 0, :, :], IR[:, 1, :, :]
            DB = NN[:, :, :, :].rearrange("p a h i -> p (a h i)").rearrange("p (h i m) -> p h i m", i=BS, m=BS)
            R = IR[:, :, :, :].rearrange("p a h i -> p (a h i)").rearrange("p (h i m) -> p h i m", i=BS, m=BS)
            Ac = s.sb("Ac", [P, HV, BS])
            Tc = s.sb("Tc", [P, HV, BS])
            pr = s.sb("pr", [P, HV, BS])
            Xc = s.sb("Xc", [P, HV, DK])
            U = s.sb("U", [P, HV, DK])
            O = s.sb("O", [P, HV, DK])
            OT = sq[:, :, :].rearrange("p (c h) d -> p c (h d)", h=2)
            xo = s.sb("xo", [P, D])
            N2t, N4, T, T16 = At, Aoff, N, Lt
            c32 = U[:, :, 0:2 * BS]
            hd = lambda bank: bank[:, :].rearrange("p (h d) -> p h d", d=DK)
            h4 = lambda bank: bank[:, :].rearrange("p (h i) -> p h i", i=P)
            gr = lambda x, q: x[:, 4 * q:4 * q + 4, :]
            with nc.Block() as block:
                @block.gpsimd
                def _(pool):
                    G.memset(KB[:, :, :, :], 0.0)
                    G.memset(QB[:, :, :, :], 0.0)
                    G.memset(hT[:, 0:PAD], 0.0)
            r.end()
            with nc.Fori(0, B) as b:
                with nc.Block(no_gpsimd_drain=True) as block:
                    @block.gpsimd
                    def _(pool):
                        G.memset(S[:, :, :], 0.0).then_inc(r["l_pz"], 1)

                    @block.vector
                    def _(dve):
                        link = linker(dve, r["l_ln"])
                        V.tensor_copy(mc[:, :], g["MODC"][:, 1, :, bass.ds(b, 1)]
                                      .rearrange("p j o -> p (j o)")).then_inc(r["l_mc"], 1)
                        layer_norm(nc, dve, link, lambda i: X[:, bass.ds(b * LT + i, 1), :]
                                   .rearrange("p o d -> p (o d)"), st, mv, rstd,
                                   lambda i: xh[:, i, :], LT, r["l_var"], r["l_rstd"]).then_inc(r["l_xn"], 1)
                        dve.wait_ge(r["l_ab"], 1)
                        pab = PB[1][:, 0:LT * 2 * HV].rearrange("p (t k h) -> p t k h", t=LT, k=2)
                        link(V.tensor_scalar(ab[:, :, :], pab[:, :, 0, :], -1.0, 80.0, ALU.mult, ALU.min))
                        link(V.tensor_tensor(sp_x[:, :, :], pab[:, :, 1, :], bcast(dtb[:, :], 1, LT), ALU.add))
                        V.scalar_tensor_tensor(sp_y[:, :, :], sp_x[:, :, :], -1.0, sp_x[:, :, :],
                                               ALU.mult, ALU.min).then_inc(r["l_y"], 1)
                        dve.wait_ge(r["l_ey"], 2)
                        link(V.tensor_scalar(ab[:, :, :], ab[:, :, :], 1.0, None, ALU.add))
                        link(V.reciprocal(gates[:, :, BE, :], ab[:, :, :]))
                        link(V.tensor_scalar(sp_s[:, :, :], sp_y[:, :, :], 2.0, None, ALU.add))
                        link(V.reciprocal(sp_s[:, :, :], sp_s[:, :, :]))
                        link(V.tensor_tensor(sp_s[:, :, :], sp_s[:, :, :], sp_y[:, :, :], ALU.mult))
                        link(V.tensor_tensor(sp_y[:, :, :], sp_s[:, :, :], sp_s[:, :, :], ALU.mult))
                        link(V.tensor_scalar(sp_p[:, :, :], sp_y[:, :, :], 1.0 / 15, None, ALU.mult))
                        for n in (13, 11, 9, 7, 5, 3):
                            link(V.scalar_tensor_tensor(sp_p[:, :, :], sp_p[:, :, :], 1.0 / n, sp_y[:, :, :],
                                                        ALU.add, ALU.mult))
                        link(V.scalar_tensor_tensor(sp_p[:, :, :], sp_p[:, :, :], 1.0, sp_s[:, :, :],
                                                    ALU.add, ALU.mult))
                        link(V.tensor_scalar(sp_x[:, :, :], sp_x[:, :, :], 0.0, None, ALU.max))
                        link(V.scalar_tensor_tensor(sp_p[:, :, :], sp_p[:, :, :], 2.0, sp_x[:, :, :],
                                                    ALU.mult, ALU.add))
                        V.tensor_tensor(sp_g[:, :, :], sp_p[:, :, :], bcast(nA[:, :], 1, LT), ALU.mult)\
                            .then_inc(r["l_g"], 1)
                        dve.wait_ge(r["l_g"], 1)

                    @block.scalar
                    def _(act):
                        root(nc, act, rstd[:, :], r["l_var"], r["l_rstd"])
                        act.wait_ge(r["l_mc"], 1)
                        act.wait_ge(r["l_xT"], 1)
                        nc.scalar.activation(hT[:, PAD:PAD + L], PB[0][:, :], ACT.Identity, bias=mc[:, 0:1],
                                             scale=mc[:, 1:2]).then_inc(r["l_hT"], 1)
                        act.wait_ge(r["l_y"], 1)
                        nc.scalar.activation(ab[:, :, :], ab[:, :, :], ACT.Exp).then_inc(r["l_ey"], 1)
                        nc.scalar.activation(sp_y[:, :, :], sp_y[:, :, :], ACT.Exp).then_inc(r["l_ey"], 1)
                        act.wait_ge(r["l_g"], 1)
                        nc.scalar.activation(gates[:, :, AL, :], sp_g[:, :, :], ACT.Exp).then_inc(r["l_al"], 1)
                        act.wait_ge(r["l_cs"], 1)
                        tg = lambda x: x.rearrange("p (t h) -> p t h", t=LT)
                        nc.scalar.activation(gates[:, :, GM, :], tg(PB[2][:, 0:LT * HV]), ACT.Exp)\
                            .then_inc(r["l_gc"], 1)
                        nc.scalar.activation(gates[:, :, GC, :], tg(PB[3][:, 0:LT * HV]), ACT.Exp)\
                            .then_inc(r["l_gc"], 1)

                    @block.tensor
                    def _(pe):
                        pe.wait_ge(r["l_xn"], 1)
                        for t in range(LT):
                            last = TE_.transpose(PB[0][:, t * P:(t + 1) * P], xh[:, t, :], ident[:, :])
                        last.then_inc(r["l_xT"], 1)
                        pe.wait_ge(r["l_hT"], 1)
                        for t in range(LT):
                            last = TE_.matmul(PB[1][:, t * 2 * HV:(t + 1) * 2 * HV],
                                              hT[:, PAD + t * P:PAD + (t + 1) * P], Wab[:, :], start=True, stop=True)
                        last.then_inc(r["l_ab"], 1)
                        pe.wait_ge(r["l_g"], 1)
                        gg = sp_g[:, :, :].rearrange("p t h -> p (t h)")
                        TE_.matmul(PB[2][:, 0:LT * HV], trif[:, :], gg, start=True, stop=True)
                        TE_.matmul(PB[3][:, 0:LT * HV], onesf[:, :], gg, start=True, stop=True).then_inc(r["l_cs"], 1)
                r.end()
                with nc.Fori(0, LT) as t:
                    with nc.Block(no_gpsimd_drain=True) as block:
                        @block.scalar
                        def _(act):
                            A_ = nc.scalar.activation
                            for c in range(4):
                                act.wait_ge(s["t_qkv"], c + 1)
                                A_(qkv[:, c * 512:(c + 1) * 512], PB[c][:, :], ACT.Silu).then_inc(s["t_silu"], 1)
                            for c in range(2):
                                act.wait_ge(s["t_z"], c + 1)
                                A_(zs[:, 8 * c:8 * c + 8, :], hd(PB[4 + c]), ACT.Silu).then_inc(s["t_za"], 1)
                            act.wait_ge(s["t_ss"], 1)
                            A_(rn[:, :], rn[:, :], ACT.Sqrt).then_inc(s["t_sq"], 1)
                            act.wait_ge(s["t_tq"], 1)
                            A_(QT[:, :, :], h4(PB[0]), ACT.Copy)
                            A_(QB[0:64, :, 0, :], h4(PB[0])[0:64, :, :], ACT.Copy)
                            A_(QB[64:P, :, 1, :], h4(PB[0])[64:P, :, :], ACT.Copy).then_inc(s["t_tqa"], 1)
                            act.wait_ge(s["t_A"], HV)
                            for c in range(4):
                                last = A_(c32[32 * c:32 * c + 32, :, :], At[32 * c:32 * c + 32, :, 32 * c:32 * c + 32],
                                          ACT.Copy)
                            last.then_inc(s["t_acp"], 1)
                            for n in range(8):
                                act.wait_ge(s["t_DB"], n + 1)
                                A_(DB[:, 2 * n:2 * n + 2, :, :].rearrange("p h i m -> p (h i m)"), BB[n % 4][:, :],
                                   ACT.Copy).then_inc(s["t_DBe"], 1)
                            for q in range(Q4):
                                act.wait_ge(s["t_Tp"], q + 1)
                                A_(gr(T16, q), h4(BA[q]), ACT.Copy).then_inc(s["t_Tpe"], 1)
                            for q in range(Q4):
                                act.wait_ge(s["t_N"], q + 1)
                                A_(gr(N, q), h4(BB[q]), ACT.Copy).then_inc(s["t_Ne"], 1)
                            for q in range(Q4):
                                act.wait_ge(s["t_Nt"], q + 1)
                                act.wait_ge(s["t_Ntd"], q + 1)
                                A_(gr(Nt, q), h4(BA[q]), ACT.Copy).then_inc(s["t_Nta"], 1)
                            for q in range(Q4):
                                act.wait_ge(s["t_N2"], q + 1)
                                A_(gr(N2, q), h4(BB[q]), ACT.Copy).then_inc(s["t_N2e"], 1)
                            for q in range(Q4):
                                act.wait_ge(s["t_N2t"], q + 1)
                                A_(gr(N2t, q), h4(BA[q]), ACT.Copy).then_inc(s["t_N2te"], 1)
                            for q in range(Q4):
                                act.wait_ge(s["t_N4"], q + 1)
                                A_(gr(N4, q), h4(BA[q]), ACT.Copy).then_inc(s["t_N4e"], 1)
                            for q in range(Q4):
                                act.wait_ge(s["t_T"], q + 1)
                                A_(gr(T, q), h4(BA[q]), ACT.Copy).then_inc(s["t_Te"], 1)
                            act.wait_ge(s["t_on"], 1)
                            A_(rn[:, :], rn[:, :], ACT.Sqrt).then_inc(s["t_or"], 1)
                            for c in range(2):
                                act.wait_ge(s["t_oT"], c + 1)
                                A_(OT[:, 4 * c:4 * c + 4, :], h4(BB[c]), ACT.Copy).then_inc(s["t_oTe"], 1)

                        @block.gpsimd
                        def _(pool):
                            link = linker(pool, s["t_pl"])
                            for q in range(Q4):
                                pool.wait_ge(s["t_L"], q + 1)
                                G.affine_select(out=gr(At, q), in_=gr(Lt, q), compare_op=ALU.is_gt, fill=0.0,
                                                base=0, pattern=[[0, 4], [1, P]], channel_multiplier=-1)\
                                    .then_inc(s["t_Ls"], 1)
                            pool.wait_ge(s["t_acp"], 1)
                            link(G.tensor_scalar(Ac[:, :, :], c32[:, :, 0:BS], hm[:, 0:1], None, ALU.mult))
                            link(G.tensor_scalar(pr[:, :, :], c32[:, :, BS:2 * BS], hm[:, 1:2], None, ALU.mult))
                            link(G.tensor_tensor(Ac[:, :, :], Ac[:, :, :], pr[:, :, :], ALU.add))
                            for q in range(Q4):
                                G.tensor_tensor(R[:, 4 * q:4 * q + 4, :, :], bcast(gr(Ac, q), 3, BS),
                                                bcast(bcast(d16[:, :], 1, BS), 1, 4), ALU.mult).then_inc(s["t_R"], 1)
                            pool.wait_ge(s["t_za"], 2)
                            link(G.tensor_tensor(zs[:, :, :], zs[:, :, :], bcast(nw[:, :], 1, HV), ALU.mult))

                        @block.tensor
                        def _(pe):
                            mm = TE_.matmul
                            pe.wait_ge(s["t_h"], 1)
                            for c in range(4):
                                for i in range(KS):
                                    last = mm(PB[c][:, :], hw[:, i:i + P], Wc[:, i, c * 512:(c + 1) * 512],
                                              start=(i == 0), stop=(i == KS - 1))
                                last.then_inc(s["t_qkv"], 1)
                            for c in range(2):
                                mm(PB[4 + c][:, :], hw[:, PAD:PAD + P], Wz[:, c * 512:(c + 1) * 512],
                                   start=True, stop=True).then_inc(s["t_z"], 1)
                            for q, bank in enumerate((PB[6], PB[7], PB[4], PB[5])):
                                if q >= 2:
                                    pe.wait_ge(s["t_za"], q - 1)
                                for h in range(4):
                                    last = mm(bank[:, h * P:(h + 1) * P], bcast(gs[:, AL, 4 * q + h], 1, P),
                                              identz[:, :], start=True, stop=True)
                                last.then_inc(s["t_al"], 1)
                            pe.wait_ge(s["t_qkn"], 1)
                            for k in range(4):
                                TE_.transpose(PB[0][:, k * P:(k + 1) * P], qkv[:, k * P:(k + 1) * P], ident[:, :])
                                last = TE_.transpose(PB[1][:, k * P:(k + 1) * P],
                                                     qkv[:, KD + k * P:KD + (k + 1) * P], ident[:, :])
                            last.then_inc(s["t_tq"], 1)
                            pe.wait_ge(s["t_tqa"], 1)
                            pe.wait_ge(s["t_tqd"], 1)
                            pe.wait_ge(s["t_silu"], 4)
                            for q in range(Q4):
                                if q == 2:
                                    pe.wait_ge(s["t_L"], 2)
                                mm(BB[q][:, 0:256], KT[:, q, :], KB[:, q, :, :].rearrange("p a i -> p (a i)"),
                                   start=True, stop=True)
                                mm(BB[q][:, 256:512], KT[:, q, :], QB[:, q, :, :].rearrange("p a i -> p (a i)"),
                                   start=True, stop=True).then_inc(s["t_kq"], 1)

                            def product(q, bank, lhsT, rhs, sem):
                                for h in range(4 * q, 4 * q + 4):
                                    last = mm(bank[q][:, (h % 4) * P:(h % 4 + 1) * P], lhsT[:, h, :], rhs[:, h, :],
                                              start=True, stop=True)
                                last.then_inc(sem, 1)

                            def turn(q, bank, x, sem):
                                for h in range(4 * q, 4 * q + 4):
                                    last = TE_.transpose(bank[q][:, (h % 4) * P:(h % 4 + 1) * P], x[:, h, :],
                                                         ident[:, :])
                                last.then_inc(sem, 1)
                            pe.wait_ge(s["t_L"], 4)
                            for q in range(Q4):
                                pe.wait_ge(s["t_A"], 4 * q + 4)
                                turn(q, BA, At, s["t_AT"])
                            for n in range(8):
                                pe.wait_ge(s["t_R"], n // 2 + 1)
                                if n < 4:
                                    pe.wait_ge(s["t_P"], n + 1)
                                else:
                                    pe.wait_ge(s["t_DBe"], n - 3)
                                mm(BB[n % 4][:, :], bone[:, :],
                                   R[:, 2 * n:2 * n + 2, :, :].rearrange("p h i m -> p (h i m)"),
                                   start=True, stop=True).then_inc(s["t_DB"], 1)
                            pe.wait_ge(s["t_T16"], 1)
                            for q in range(Q4):
                                pe.wait_ge(s["t_ATe"], q + 1)
                                turn(q, BA, Tt16, s["t_Tp"])
                            pe.wait_ge(s["t_DBe"], 8)
                            for q in range(Q4):
                                product(q, BB, Tt16, Aoff, s["t_N"])
                            for q in range(Q4):
                                pe.wait_ge(s["t_Tpe"], q + 1)
                                product(q, BA, Aoff, Tt16, s["t_Nt"])
                            for q in range(Q4):
                                pe.wait_ge(s["t_Ne"], q + 1)
                                pe.wait_ge(s["t_Nta"], q + 1)
                                product(q, BB, Nt, N, s["t_N2"])
                            for q in range(Q4):
                                product(q, BA, N, Nt, s["t_N2t"])
                            for q in range(Q4):
                                pe.wait_ge(s["t_N2e"], q + 1)
                                pe.wait_ge(s["t_Ntd"], q + 1)
                                product(q, BB, N2, IN, s["t_R1"])
                            for q in range(Q4):
                                pe.wait_ge(s["t_N2te"], q + 1)
                                product(q, BA, N2t, N2, s["t_N4"])
                            for q in range(Q4):
                                pe.wait_ge(s["t_N4e"], q + 1)
                                pe.wait_ge(s["t_R1e"], q + 1)
                                product(q, BB, N4, IN, s["t_R2"])
                            for q in range(Q4):
                                pe.wait_ge(s["t_R2e"], q + 1)
                                product(q, BA, T16, IN, s["t_T"])
                            pe.wait_ge(s["t_Te"], 4)
                            half = lambda q: slice(q % 2 * 256, q % 2 * 256 + 256)
                            for q in range(Q4):
                                last = mm(BA[q // 2][:, half(q)], KT[:, q, :], S[:, q, :], start=True, stop=True)
                                if q % 2:
                                    last.then_inc(s["t_KS"], 1)
                            for q in range(Q4):
                                last = mm(BA[2 + q // 2][:, half(q)], QT[:, q, :], S[:, q, :], start=True, stop=True)
                                if q % 2:
                                    last.then_inc(s["t_QS"], 1)
                            for c in range(2):
                                pe.wait_ge(s["t_X"], c + 1)
                                for h in range(8 * c, 8 * c + 8):
                                    last = mm(BB[c][:, h % 8 * DK:(h % 8 + 1) * DK], T[:, h, :], Xc[:, h, :],
                                              start=True, stop=True)
                                last.then_inc(s["t_W"], 1)
                            for c in range(2):
                                pe.wait_ge(s["t_U"], c + 1)
                                for h in range(8 * c, 8 * c + 8):
                                    last = mm(BB[2 + c][:, h % 8 * DK:(h % 8 + 1) * DK], Pt[:, h, :], U[:, h, :],
                                              start=True, stop=True)
                                last.then_inc(s["t_PU"], 1)
                            for c in range(2):
                                pe.wait_ge(s["t_U2"], c + 1)
                                for q in (2 * c, 2 * c + 1):
                                    last = mm(BA[c][:, half(q)], qkv[:, KD + q * P:KD + (q + 1) * P],
                                              Xc[:, 4 * q:4 * q + 4, :].rearrange("p h d -> p (h d)"),
                                              start=True, stop=True)
                                last.then_inc(s["t_dS"], 1)
                            pe.wait_ge(s["t_of"], 1)
                            for c in range(8):
                                last = TE_.transpose(BB[c // 4][:, c % 4 * P:(c % 4 + 1) * P],
                                                     O[:, 2 * c:2 * c + 2, :].rearrange("p h d -> p (h d)"),
                                                     ident[:, :])
                                if c % 4 == 3:
                                    last.then_inc(s["t_oT"], 1)
                            for c in range(8):
                                pe.wait_ge(s["t_oTe"], c // 4 + 1)
                                last = mm(BA[2][:, 0:D], OT[:, c, :], Wo[:, c, :], start=(c == 0), stop=(c == 7))
                            last.then_inc(s["t_out"], 1)

                        @block.vector
                        def _(dve):
                            link = linker(dve, s["t_v"])
                            V.tensor_copy(gs[:, :, :], gates[:, bass.ds(t, 1), :, :].rearrange("p o k h -> p (o k) h"))
                            V.tensor_copy(hw[:, :], hT[:, bass.ds(t * P, PAD + P)]).then_inc(s["t_h"], 1)
                            qk = qkv[:, 0:2 * KD].rearrange("p (h d) -> p h d", d=DK)
                            dve.wait_ge(s["t_silu"], 2)
                            link(V.tensor_tensor(sq[:, :, :], qk, qk, ALU.mult))
                            link(V.tensor_reduce(rn[:, :], sq[:, :, :], AX.X, ALU.add))
                            V.tensor_scalar(rn[:, :], rn[:, :], EPS1, None, ALU.add).then_inc(s["t_ss"], 1)
                            for q, bank in enumerate((PB[6], PB[7], PB[4], PB[5])):
                                dve.wait_ge(s["t_al"], q + 1)
                                V.tensor_tensor_scan(gr(Lt, q).rearrange("p h i -> p (h i)"), bank[:, :],
                                                     I4[:, :, :].rearrange("p h i -> p (h i)"), 0.0,
                                                     ALU.mult, ALU.add).then_inc(s["t_L"], 1)
                            dve.wait_ge(s["t_sq"], 1)
                            link(V.reciprocal(rn[:, :], rn[:, :]))
                            link(V.tensor_scalar(rn[:, 0:HK], rn[:, 0:HK], SQ, None, ALU.mult))
                            V.tensor_tensor(qk, qk, bcast(rn[:, :], 2, DK), ALU.mult).then_inc(s["t_qkn"], 1)
                            dve.wait_ge(s["t_tq"], 1)
                            V.tensor_copy(KT[:, :, :], h4(PB[1]))
                            V.tensor_copy(KB[0:64, :, 0, :], h4(PB[1])[0:64, :, :])
                            V.tensor_copy(KB[64:P, :, 1, :], h4(PB[1])[64:P, :, :]).then_inc(s["t_tqd"], 1)
                            for q in range(Q4):
                                dve.wait_ge(s["t_kq"], q + 1)
                                dve.wait_ge(s["t_Ls"], q + 1)
                                for h in range(4 * q, 4 * q + 4):
                                    k = h // 2 % 2
                                    V.scalar_tensor_tensor(At[:, h, :], BB[q][:, k * P:(k + 1) * P],
                                                           gs[:, BE, h:h + 1], At[:, h, :], ALU.mult, ALU.mult)\
                                        .then_inc(s["t_A"], 1)
                            for q in range(Q4):
                                kq = BB[q][:, 256:512].rearrange("p (k i) -> p k i", k=2)
                                f2 = lambda x: gr(x, q).rearrange("p (k v) i -> p k v i", v=2)
                                V.tensor_tensor(f2(Pt), bcast(kq, 2, 2), f2(Lt), ALU.mult).then_inc(s["t_P"], 1)
                            link(V.tensor_copy(dl[:, :], Lt[:, :, P - 1]))
                            for q in range(Q4):
                                dve.wait_ge(s["t_AT"], q + 1)
                                V.tensor_tensor(gr(Aoff, q), h4(BA[q]), bcast(offm[:, :], 1, 4), ALU.mult)\
                                    .then_inc(s["t_ATe"], 1)
                            link(V.tensor_copy(Tc[:, :, :], bcast(d16[:, :], 1, HV)))
                            dve.wait_ge(s["t_DBe"], 8)
                            for i in range(BS - 1):
                                n = BS - 1 - i
                                link(V.tensor_tensor(pr[:, :, 0:n], DB[:, :, i + 1:BS, i],
                                                     bcast(Tc[:, :, i], 2, n), ALU.mult))
                                link(V.tensor_tensor(Tc[:, :, i + 1:BS], Tc[:, :, i + 1:BS], pr[:, :, 0:n],
                                                     ALU.subtract))
                            V.tensor_tensor(Tt16[:, :, :].rearrange("p h (c i) -> p h c i", i=BS),
                                            bcast(Tc[:, :, :], 2, P // BS), bcast(bcast(bm[:, :], 2, BS), 1, HV),
                                            ALU.mult).then_inc(s["t_T16"], 1)
                            for q in range(Q4):
                                dve.wait_ge(s["t_Nt"], q + 1)
                                V.tensor_tensor(gr(IN, q), I4[:, :, :], h4(BA[q]), ALU.subtract)\
                                    .then_inc(s["t_Ntd"], 1)
                            for q in range(Q4):
                                dve.wait_ge(s["t_R1"], q + 1)
                                dve.wait_ge(s["t_Ntd"], q + 1)
                                V.tensor_tensor(gr(IN, q), gr(IN, q), h4(BB[q]), ALU.add).then_inc(s["t_R1e"], 1)
                            for q in range(Q4):
                                dve.wait_ge(s["t_R2"], q + 1)
                                dve.wait_ge(s["t_R1e"], q + 1)
                                V.tensor_tensor(gr(IN, q), gr(IN, q), h4(BB[q]), ALU.add).then_inc(s["t_R2e"], 1)
                            v = qkv[:, 2 * KD:CD].rearrange("p (h d) -> p h d", d=DK)
                            e8 = lambda x, c: x[:, 8 * c:8 * c + 8, :]
                            gb_ = lambda k, c: bcast(gs[:, k, 8 * c:8 * c + 8], 2, DK)
                            for c in range(2):
                                dve.wait_ge(s["t_KS"], c + 1)
                                link(V.tensor_tensor(e8(Xc, c), hd(BA[c]), gb_(GM, c), ALU.mult))
                                V.tensor_tensor(e8(Xc, c), e8(v, c), e8(Xc, c), ALU.subtract).then_inc(s["t_X"], 1)
                            for c in range(2):
                                dve.wait_ge(s["t_W"], c + 1)
                                V.tensor_tensor(e8(U, c), hd(BB[c]), gb_(BE, c), ALU.mult).then_inc(s["t_U"], 1)
                            dve.wait_ge(s["t_U"], 2)
                            for c in range(2):
                                V.tensor_tensor(e8(Xc, c), e8(U, c), bcast(dl[:, 8 * c:8 * c + 8], 2, DK),
                                                ALU.mult).then_inc(s["t_U2"], 1)
                            for c in range(2):
                                dve.wait_ge(s["t_QS"], c + 1)
                                link(V.tensor_tensor(e8(O, c), hd(BA[2 + c]), gb_(GM, c), ALU.mult))
                            for c in range(2):
                                dve.wait_ge(s["t_PU"], c + 1)
                                link(V.tensor_tensor(e8(O, c), e8(O, c), hd(BB[2 + c]), ALU.add))
                            link(V.tensor_tensor(sq[:, :, :], O[:, :, :], O[:, :, :], ALU.mult))
                            link(V.tensor_reduce(rn[:, :], sq[:, :, :], AX.X, ALU.add))
                            V.tensor_scalar(rn[:, :], rn[:, :], 1.0 / DK, EPS1, ALU.mult, ALU.add)\
                                .then_inc(s["t_on"], 1)
                            Sh = S[:, :, :].rearrange("p q (h d) -> p (q h) d", d=DK)
                            link(V.tensor_tensor(Sh, Sh, bcast(gs[:, GC, :], 2, DK), ALU.mult))
                            for c in range(2):
                                dve.wait_ge(s["t_dS"], c + 1)
                                for k in range(2):
                                    rows_, cols = slice(64 * k, 64 * k + 64), slice(P * k, P * k + P)
                                    d = BA[c][rows_, :].rearrange("p (q n) -> p q n", q=2)[:, :, cols]
                                    o = S[rows_, 2 * c:2 * c + 2, cols]
                                    link(V.tensor_tensor(o, o, d, ALU.add))
                            dve.wait_ge(s["t_or"], 1)
                            link(V.reciprocal(rn[:, :], rn[:, :]))
                            link(V.tensor_tensor(O[:, :, :], O[:, :, :], bcast(rn[:, :], 2, DK), ALU.mult))
                            dve.wait_ge(s["t_pl"], 4)
                            V.tensor_tensor(O[:, :, :], O[:, :, :], zs[:, :, :], ALU.mult).then_inc(s["t_of"], 1)
                            dve.wait_ge(s["t_out"], 1)
                            link(V.tensor_tensor(xo[:, :], BA[2][:, 0:D],
                                                 g["MODB"][:, bass.ds(b, 1), GA, :].rearrange("p o d -> p (o d)"),
                                                 ALU.mult))
                            xt = X[:, bass.ds(b * LT + t, 1), :].rearrange("p o d -> p (o d)")
                            link(V.tensor_tensor(xt, xt, xo[:, :], ALU.add))
                    s.end()


def network(nc, out, a):
    with ExitStack() as ctx:
        g = globals_(nc, ctx)
        setup(nc, g, a)
        modulate(nc, g, a, 0)
        attention0(nc, g, a)
        experts0(nc, g, a)
        modulate(nc, g, a, 1)
        delta1(nc, g, a)
        experts1(nc, g, a)
        store(nc, g, out)


def kernel(**inputs):
    import numpy as _np
    import concourse.bacc as _bacc
    from concourse import mybir as _mybir
    from concourse.bass_utils import run_bass_kernel_spmd as _run

    nc = _bacc.Bacc("TRN2", target_bir_lowering=False, num_devices=1)
    arrays, args = {}, {}
    for name in sorted(inputs):
        v = _np.ascontiguousarray(inputs[name])
        arrays[f"in_{name}"] = v
        args[name] = nc.dram_tensor(f"in_{name}", v.shape, _mybir.dt.from_np(v.dtype), kind="ExternalInput").ap()
    out = nc.dram_tensor("out_0", (B, L, D), _mybir.dt.from_np(_np.dtype("float32")), kind="ExternalOutput").ap()
    network(nc, out, args)
    nc.compile()
    r = _run(nc, [arrays], core_ids=[0])
    return r.results[0]["out_0"]
```
